# Optimizing a Trainium2 kernel written in Bass

```python
import numpy as np
import jax
import jax.numpy as jnp

def _softmax(x, axis=-1):
    return jax.nn.softmax(x, axis=axis)
def _gelu(x):
    return jax.nn.gelu(x, approximate=True)
def _silu(x):
    return jax.nn.silu(x)
def _sigmoid(x):
    return jax.nn.sigmoid(x)
def _layernorm(x, axis=-1, eps=1e-5):
    m = jnp.mean(x, axis=axis, keepdims=True)
    v = jnp.var(x, axis=axis, keepdims=True)
    return (x - m) / jnp.sqrt(v + eps)
def _scatter_add(tgt, idx, src, axis=0):
    return tgt.at[idx].add(src)
def _segment_sum(src, seg, n):
    return jax.ops.segment_sum(src, seg, n)

kernel_name = 'mk_adj_resnorm_d2_adj_512_10e2f9'

def setup_inputs(seed: int = 0):
    np.random.seed(seed)
    _w = jnp.asarray
    def _rec_inputs():
        import jax
        import jax.numpy as jnp
        _gk = jax.random.key(seed)
        x = -0.0005207 + 1.001 * jax.random.normal(jax.random.fold_in(_gk, 1), (16, 1024, 512), jnp.float32)
        _w = (1.0 + jnp.arange(1024, dtype=jnp.float32)) ** -0.5
        _w = _w / _w.mean()
        _pij = jnp.clip(0.015625 * _w[:, None] * _w[None, :], 0.0, 1.0)
        _a = jax.random.uniform(jax.random.fold_in(_gk, 2), (16, 1024, 1024)) < _pij
        _a = jnp.logical_or(_a, jnp.eye(1024, dtype=bool))
        _af = _a.astype(jnp.float32)
        adj = _af
        return x, adj
    x, adj = _rec_inputs()
    def _L0_gnn_setup():
        import jax, jax.numpy as jnp
        import numpy as np
        N = 4096
        F_IN = 512
        UNITS = 64
        HEADS = 8
        NEG_BIG = -10000000000.0
        key = jax.random.key(seed)
        ks = jax.random.split(key, 7)
        X = jax.random.normal(ks[0], (1, N, F_IN), dtype=jnp.float32)
        A = (jax.random.uniform(ks[1], (1, N, N)) < 0.008).astype(jnp.float32)
        A = jnp.maximum(A, jnp.eye(N, dtype=jnp.float32)[None])
        glorot = lambda k, shp: jax.random.uniform(k, shp, jnp.float32, -1.0, 1.0) * jnp.sqrt(6.0 / (shp[-2] + shp[-1]))
        W = glorot(ks[2], (HEADS, F_IN, UNITS))
        b = jnp.zeros((HEADS, UNITS), dtype=jnp.float32)
        a_self = glorot(ks[3], (HEADS, UNITS, 1))[..., 0]
        a_neigh = glorot(ks[4], (HEADS, UNITS, 1))[..., 0]
        return {'X': X, 'A': A, 'W': W, 'b': b, 'a_self': a_self, 'a_neigh': a_neigh}
    _L0_gnn_all = _L0_gnn_setup()
    _L0_gnn_in = {k: v for k, v in _L0_gnn_all.items() if k in ('W', 'b', 'a_self', 'a_neigh', )}
    del _L0_gnn_all

    def _L1_gnn_setup():
        import jax, jax.numpy as jnp
        import numpy as np
        EPS = 1e-06
        key = jax.random.key(seed)
        k1, k2, k3 = jax.random.split(key, 3)
        B, N, F, O = (8, 4096, 512, 512)
        x = jax.random.normal(k1, (B, N, F), dtype=jnp.float32)
        adj = jax.random.uniform(k2, (B, N, N), dtype=jnp.float32)
        W = jax.random.normal(k3, (O, 2 * F), dtype=jnp.float32) * (1.0 / np.sqrt(2 * F))
        return {'x': x, 'adj': adj, 'W': W}
    _L1_gnn_all = _L1_gnn_setup()
    _L1_gnn_in = {k: v for k, v in _L1_gnn_all.items() if k in ('W', )}
    del _L1_gnn_all

    return {
        "x": x,
        "adj": adj,
        "L0_gnn_W": _L0_gnn_in["W"],
        "L0_gnn_b": _L0_gnn_in["b"],
        "L0_gnn_a_self": _L0_gnn_in["a_self"],
        "L0_gnn_a_neigh": _L0_gnn_in["a_neigh"],
        "L1_gnn_W": _L1_gnn_in["W"],
    }

def reference(x, adj, L0_gnn_W, L0_gnn_b, L0_gnn_a_self, L0_gnn_a_neigh, L1_gnn_W):
    import jax
    import jax.numpy as jnp
    def _L0_gnn_ref(X, A, W, b, a_self, a_neigh):
        import jax, jax.numpy as jnp
        import numpy as np
        N = 4096
        F_IN = 512
        UNITS = 64
        HEADS = 8
        NEG_BIG = -10000000000.0
        feats = jnp.einsum('bnf,hfu->bhnu', X, W)
        e_self = jnp.einsum('bhnu,hu->bhn', feats, a_self)
        e_neigh = jnp.einsum('bhnu,hu->bhn', feats, a_neigh)
        dense = e_self[..., :, None] + e_neigh[..., None, :]
        dense = jax.nn.leaky_relu(dense, negative_slope=0.2)
        dense = dense + NEG_BIG * (1.0 - A[:, None, :, :])
        att = jax.nn.softmax(dense, axis=-1)
        out = jnp.einsum('bhij,bhju->bhiu', att, feats) + b[None, :, None, :]
        out = out.transpose(0, 2, 1, 3).reshape(X.shape[0], X.shape[1], HEADS * UNITS)
        return jax.nn.relu(out)

    def _L1_gnn_ref(x, adj, W):
        import jax, jax.numpy as jnp
        import numpy as np
        EPS = 1e-06
        deg = jnp.sum(adj, axis=-1, keepdims=True)
        agg = jnp.einsum('bij,bjf->bif', adj, x) / jnp.maximum(deg, EPS)
        cat = jnp.concatenate([x, agg], axis=2)
        out = jnp.einsum('bnf,of->bno', cat, W)
        return jax.nn.relu(out)

    x = _layernorm(x + _L0_gnn_ref(x, adj, L0_gnn_W, L0_gnn_b, L0_gnn_a_self, L0_gnn_a_neigh), axis=-1)
    x = _layernorm(x + _L1_gnn_ref(x, adj, L1_gnn_W), axis=-1)
    return x


_drawn_inputs = setup_inputs


def setup_inputs(seed=0):
    import zlib

    import numpy as np

    out = dict(_drawn_inputs(seed))
    spreads = {'L0_gnn_b': (0.0, 0.1)}
    factors = {}
    for name, (base, spread) in spreads.items():
        noise = np.random.default_rng([zlib.crc32(name.encode()), seed]).standard_normal(out[name].shape)
        drawn = base * np.exp(spread * noise) if base else spread * noise
        out[name] = jnp.asarray(drawn.astype(out[name].dtype))
    for name, factor in factors.items():
        out[name] = (out[name] * factor).astype(out[name].dtype)
    return out
```

```python
from contextlib import ExitStack

import concourse.bass as bass
from concourse import mybir

F32 = mybir.dt.float32
F32R = mybir.dt.float32r
BF16 = mybir.dt.bfloat16
F16 = mybir.dt.float16
ALU = mybir.AluOpType
ACT = mybir.ActivationFunctionType
AX = mybir.AxisListType

P = 128
LN_EPS = 1e-5
DEG_EPS = 1e-6
SLOPE = 0.2
STEP = 2.0 ** 100
X1_SCALE = 2.0 ** 11
MASK_SLOTS = 6
STEP_SLOTS = 3
PARTS = 3


class Signal:

    def __init__(self, sem, per_batch):
        self.sem, self.per_batch = sem, per_batch

    def wait(self, engine, batch, count):
        assert 0 < count <= self.per_batch
        engine.wait_ge(self.sem, batch * self.per_batch + count)


def gat_sage_kernel(nc, x, adj, gat_w, gat_b, gat_self, gat_neigh, sage_w, out):
    B, N, D = x.shape
    H, _, U = gat_w.shape
    T = N // P
    KC = D // P
    HALF = T // 2
    U1 = U + 1
    HU = H * U
    SC = 2 * H
    BANK = 512
    TPB = BANK // P
    QPB = 3
    GROUPS = (T + QPB - 1) // QPB
    POOL_KEYS = (2, 6)
    NPOOL = len(POOL_KEYS)
    NDVE = T - NPOOL

    with ExitStack() as ctx:
        def sb(name, shape, dt):
            return ctx.enter_context(nc.sbuf_tensor(name, shape, dt))

        def sem(name):
            return ctx.enter_context(nc.semaphore(name))

        ident = sb("ident", [P, P], F32)
        ones_bf = sb("ones_bf", [P, 1], BF16)
        ones16 = sb("ones16", [SC, P], F32)
        pick = sb("pick", [48, H, P], F32R)
        bias_bc = sb("bias_bc", [P, HU], F32)
        w0h = sb("w0h", [P, KC, HU], F32R)
        w0l = sb("w0l", [P, KC, HU], F32R)
        wah = sb("wah", [P, KC, P], F32R)
        wal = sb("wal", [P, KC, P], F32R)
        w1h = sb("w1h", [P, 2 * KC, D], F32R)
        w1l = sb("w1l", [P, 2 * KC, D], F32R)
        xs = sb("xs", [P, T, D], F32)
        x1_parts = sb("x1_parts", [P, 2, T, D], F16)
        x1h, x1l = x1_parts[:, 0], x1_parts[:, 1]
        pool32 = x1_parts[:, :, :, :].rearrange("p k t d -> p (k t d)").bitcast(F32)

        def head_buffer(k):
            return pool32[:, k * 2 * T * U1:(k + 1) * 2 * T * U1].rearrange("p (k t u) -> p k t u", k=2, t=T)

        val32 = head_buffer(0)
        rest = head_buffer(1)
        low_sum = head_buffer(2)
        feat = sb("feat", [P, T, H, U1], F32)
        trh = sb("trh", [P, KC, HALF * P], F32R)
        trl = sb("trl", [P, KC, HALF * P], F32R)
        adj_nat = sb("adj_nat", [P, 2, N], F32)
        adj_t = sb("adj_t", [P, T, N], BF16)
        sc_row = sb("sc_row", [SC, N], F32)
        sc_hl = sb("sc_hl", [48, N], F32R)
        s_bc = sb("s_bc", [P, N], F32)
        step = sb("step", [P, STEP_SLOTS, N], BF16)
        mask = sb("mask", [P, 2, MASK_SLOTS, N], BF16)
        val = sb("val", [P, 2, PARTS, 2, T, U1], BF16)
        sc_nat = sb("sc_nat", [P, T, SC], F32)
        nmax16 = sb("nmax16", [SC, 1], F32)
        diag16 = sb("diag16", [SC, SC], F32)
        nmax = sb("nmax", [P, SC], F32)
        n_step = sb("n_step", [P, T, H], F32)
        dn = sb("dn", [P, T, H], F32)
        ts = sb("ts", [P, T, H], F32)
        ts_lo = sb("ts_lo", [P, T, H], F32)
        ts_hi = sb("ts_hi", [P, T, H], F32)
        key_w = sb("key_w", [P, 2, T, H], F32)
        qry_w = sb("qry_w", [P, 2, T, H], F32)
        rden = sb("rden", [P, T, H], F32)
        z = s_bc[:, :].rearrange("p (s d) -> p s d", s=2)
        stats = sb("stats", [P, 2, 6], F32)
        mv = sb("mv", [P, T, 2], F32)
        ve = sb("ve", [P, T], F32)
        sd = sb("sd", [P, T], F32)
        rs = sb("rs", [P, T], F32)
        mv1 = sb("mv1", [P, 2, 2], F32)
        ve1 = sb("ve1", [P, 2], F32)
        sd1 = sb("sd1", [P, 2], F32)
        rs1 = sb("rs1", [P, 2], F32)
        degc = sb("degc", [P, T], F32)
        rdeg = sb("rdeg", [P, T], F32)
        mask32 = mask[:, :, :, :].rearrange("p k s n -> p (k s n)").bitcast(F32)
        agg = mask32[:, 0:2 * D].rearrange("p (s d) -> p s d", s=2)
        y_out = mask32[:, 2 * D:4 * D].rearrange("p (s d) -> p s d", s=2)
        w_raw = feat[:, 0:4, :, :].rearrange("p a b c -> p (a b c)")[:, 0:KC * HU].rearrange(
            "p (c n) -> p c n", c=KC)
        a_bc = z
        prod = y_out
        wa32 = sb("wa32", [P, KC, SC], F32)
        sage_raw = xs[:, :, :].rearrange("p t d -> p (t d)").rearrange("p (c f) -> p c f", c=KC)
        pick32 = agg[0:48, :, :].rearrange("p s (k m) -> p (s k) m", m=P)

        bank = [ctx.enter_context(nc.psum_tensor(f"bank{k}", [P, BANK], F32)) for k in range(6)]
        pair = ctx.enter_context(nc.psum_tensor("pair", [P, 2 * BANK], F32))
        bank += [pair[:, 0:BANK], pair[:, BANK:2 * BANK]]

        w_in = [sem(f"w_in{k}") for k in range(4)]
        pool_const, consts = sem("pool_const"), sem("consts")
        w_ready, w1_ps, w1_hi, w1_lo, wa_step = (
            sem("w_ready"), sem("w1_ps"), sem("w1_hi"), sem("w1_lo"), sem("wa_step"))
        x_in = [Signal(sem(f"x_in{t}"), 16) for t in range(T)]
        a_in = [sem(f"a_in{s}") for s in range(2)]
        y_stored = [sem(f"y_stored{s}") for s in range(2)]

        def signal(name, per_batch):
            return Signal(sem(name), per_batch)

        xt_ps = signal("xt_ps", T)
        xt_hi = signal("xt_hi", T)
        xt_lo = signal("xt_lo", T)
        at_ps = signal("at_ps", 2 * T)
        at_act = signal("at_act", T)
        at_dve = signal("at_dve", T)
        ft_ps = signal("ft_ps", T)
        ft_sb = signal("ft_sb", T)
        sc_ps = signal("sc_ps", 2)
        sc_f32 = signal("sc_f32", 2)
        sc_hi = signal("sc_hi", 2)
        sc_lo = signal("sc_lo", 2)
        nat_ps = signal("nat_ps", 1)
        nat_sb = signal("nat_sb", 1)
        diag_ok = signal("diag_ok", 1)
        max_ps = signal("max_ps", 1)
        weights_in = signal("weights_in", 4)
        weights = signal("weights", 4)
        chain = signal("chain", 6 + 4 * T)
        sb_ps = signal("sb_ps", H)
        sb_sb = signal("sb_sb", H)
        stepped = signal("stepped", H * T)
        mask1 = signal("mask1", H * T)
        mask2_dve = signal("mask2_dve", H * NDVE)
        mask2_pool = signal("mask2_pool", H * NPOOL)
        mask_used = signal("mask_used", H * (T - 1))
        val_f32 = signal("val_f32", 2 * H)
        val_p0 = signal("val_p0", H)
        val_rest = signal("val_rest", H)
        val_p1 = signal("val_p1", H)
        val_p2 = signal("val_p2", H)
        sums_ps = signal("sums_ps", H * GROUPS)
        low_ok = signal("low_ok", H * GROUPS)
        head_ok = signal("head_ok", H * GROUPS)
        deg_ps = signal("deg_ps", 1)
        deg_max = signal("deg_max", 1)
        rdeg_ok = signal("rdeg_ok", 1)
        ln0_att = signal("ln0_att", T)
        ln0_bias = signal("ln0_bias", T)
        ln0_sum = signal("ln0_sum", T)
        ln0_mv = signal("ln0_mv", T)
        ln0_ve = signal("ln0_ve", 1)
        ln0_sd = signal("ln0_sd", 1)
        x1_ok = signal("x1_ok", T)
        x1_hi = signal("x1_hi", T)
        x1_lo = signal("x1_lo", T)
        agg_ps = signal("agg_ps", T)
        agg_sb = signal("agg_sb", T)
        x1t_ps = signal("x1t_ps", T)
        x1t_hi = signal("x1t_hi", T)
        x1t_lo = signal("x1t_lo", T)
        aggt_ps = signal("aggt_ps", T)
        aggt_hi = signal("aggt_hi", T)
        aggt_lo = signal("aggt_lo", T)
        o_ps = signal("o_ps", T)
        res_ok = signal("res_ok", T)
        ln1_ve = signal("ln1_ve", T)
        ln1_sd = signal("ln1_sd", T)
        y_ok = signal("y_ok", T)

        def rows(v):
            return v.rearrange("h u -> (h u)").partition_broadcast(P)

        def col(c):
            return slice(c * P, (c + 1) * P)

        N_CONST = 7
        turnstile = sem("turnstile")

        def stand(engine):
            engine.sem_inc(turnstile, 1)

        block = ctx.enter_context(nc.Block())

        @block.sync
        def _(sp):
            for c in range(KC):
                sp.dma_start(w_raw[:, c, :].rearrange("p (h u) -> p h u", h=H),
                             gat_w[:, col(c), :].rearrange("h p u -> p h u")).then_inc(w_in[0], 16)
            sp.dma_start(a_bc[:, 0, :], rows(gat_self)).then_inc(w_in[1], 16)
            sp.dma_start(a_bc[:, 1, :], rows(gat_neigh)).then_inc(w_in[1], 16)
            sp.dma_start(bias_bc[:, :], rows(gat_b)).then_inc(w_in[2], 16)
            sp.dma_start(sage_raw, sage_w.rearrange("(c p) f -> p c f", p=P)).then_inc(w_in[3], 16)
            sp.sem_inc(y_stored[0], 16)
            sp.sem_inc(y_stored[1], 16)

            def load_x(b, t):
                sp.dma_start(xs[:, t, :], x[b, t * P:(t + 1) * P, :]).then_inc(x_in[t].sem, 16)

            def load_adj(b, t):
                sp.dma_start(adj_nat[:, t % 2, :], adj[b, t * P:(t + 1) * P, :]).then_inc(a_in[t % 2], 16)

            def store_y(b, t):
                y_ok.wait(sp, b, t + 1)
                sp.dma_start(out[b, t * P:(t + 1) * P, :], y_out[:, t % 2, :]).then_inc(y_stored[t % 2], 16)

            def load_late_adj(b):
                for t in range(2, T):
                    at_ps.wait(sp, b, 2 * (t - 2) + 2)
                    load_adj(b, t)

            for t in range(2):
                load_adj(0, t)
            sp.wait_ge(w1_ps, 2 * KC)
            for t in range(T):
                load_x(0, t)
            load_late_adj(0)
            with sp.Fori(0, B - 1) as b:
                for t in range(2):
                    at_ps.wait(sp, b, 2 * (T - 2 + t) + 2)
                    load_adj(b + 1, t)
                for t in range(T):
                    res_ok.wait(sp, b, t + 1)
                    load_x(b + 1, t)
                    store_y(b, t)
                load_late_adj(b + 1)
            for t in range(T):
                store_y(B - 1, t)
            for s in range(2):
                sp.wait_ge(y_stored[s], 16 * (B * T // 2 + 1))

        @block.gpsimd
        def _(pool):
            pool.memset(ident[:], 0.0).then_inc(pool_const, 1)
            pool.memset(pick32, 0.0).then_inc(pool_const, 1)
            pool.wait_ge(pool_const, 2)
            pool.affine_select(out=ident[:], in_=ident[:], compare_op=ALU.not_equal, fill=1.0, base=0,
                               pattern=[[-1, P]], channel_multiplier=1).then_inc(consts, 1)
            for base in (0, -32):
                pool.affine_select(out=pick32, in_=pick32, compare_op=ALU.not_equal, fill=1.0,
                                   base=base, pattern=[[-1, H], [0, P]],
                                   channel_multiplier=1).then_inc(pool_const, 1)
                pool.wait_ge(pool_const, 3 if base == 0 else 4)
            pool.tensor_copy(pick[:], pick32).then_inc(consts, 1)
            pool.memset(ones16[:], 1.0).then_inc(consts, 1)
            pool.memset(ones_bf[:], 1.0).then_inc(consts, 1)
            pool.memset(sc_hl[:].bitcast(F32), 0.0).then_inc(consts, 1)
            pool.memset(wah[:].bitcast(F32), 0.0).then_inc(consts, 1)
            pool.memset(wal[:].bitcast(F32), 0.0).then_inc(consts, 1)
            pool.wait_ge(w_in[2], 16)

            def value_rest(b, h):
                val_f32.wait(pool, b, 2 * h + 2)
                val_p0.wait(pool, b, h + 1)
                pool.tensor_tensor(rest, val32, val[:, h % 2, 0], ALU.subtract).then_inc(val_rest.sem, 1)

            with pool.Fori(0, B) as b:
                value_rest(b, 0)
                for h in range(H):
                    for i, jt in enumerate(POOL_KEYS):
                        g = h * T + jt
                        mask1.wait(pool, b, g + 1)
                        pool.tensor_tensor(mask[:, 1, g % MASK_SLOTS], adj_t[:, jt, :],
                                           mask[:, 0, g % MASK_SLOTS],
                                           ALU.subtract).then_inc(mask2_pool.sem, 1)
                        if i == 0 and h + 1 < H:
                            value_rest(b, h + 1)
                for t in range(T):
                    ln0_att.wait(pool, b, t + 1)
                    pool.tensor_tensor(z[:, t % 2], z[:, t % 2], bias_bc[:], ALU.add).then_inc(ln0_bias.sem, 1)

        @block.scalar
        def _(act):
            def copy(o, i, s, scale=1.0):
                act.activation(o, i, ACT.Copy, scale=scale).then_inc(s, 1)

            for c in range(2 * KC):
                act.wait_ge(w1_ps, c + 1)
                copy(w1h[:, c, :], bank[c % 2][:], w1_hi)

            def value_p0(b, h):
                val_f32.wait(act, b, 2 * h + 2)
                copy(val[:, h % 2, 0], val32, val_p0.sem)

            def value_p1(b, h):
                val_rest.wait(act, b, h + 1)
                copy(val[:, h % 2, 1], rest, val_p1.sem)

            def low_sums(b, h):
                for k in range(GROUPS):
                    sums_ps.wait(act, b, h * GROUPS + k + 1)
                    qs = range(k * QPB, min(T, (k + 1) * QPB))
                    for i, q in enumerate(qs):
                        at = i * 2 * U1 + U1
                        ins = act.activation(low_sum[:, h % 2, q, :], bank[3 * (h % 2) + k][:, at:at + U1],
                                             ACT.Copy, scale=qry_w[:, 1, q, h:h + 1])
                    ins.then_inc(low_ok.sem, 1)

            with act.Fori(0, B) as b:
                for t in range(T):
                    xt_ps.wait(act, b, t + 1)
                    if t == HALF:
                        sc_ps.wait(act, b, 1)
                    c = t % HALF
                    copy(trh[:, :, col(c)], bank[t % 2][:].rearrange("p (k n) -> p k n", k=KC), xt_hi.sem)
                    at_ps.wait(act, b, 2 * t + 1)
                    copy(adj_t[:, 0:TPB, col(t)], bank[2][:].rearrange("p (k n) -> p k n", k=TPB), at_act.sem)
                    if t >= 1:
                        ft_ps.wait(act, b, t)
                        copy(feat[:, t - 1, :, 0:U], bank[4 + (t - 1) % 2][:].rearrange("p (h u) -> p h u", h=H),
                             ft_sb.sem)
                    if t == HALF or t == T - 1:
                        i = 0 if t == HALF else 1
                        if i == 1:
                            ft_ps.wait(act, b, T)
                            copy(feat[:, T - 1, :, 0:U],
                                 bank[4 + (T - 1) % 2][:].rearrange("p (h u) -> p h u", h=H), ft_sb.sem)
                        sc_ps.wait(act, b, i + 1)
                        half = slice(i * HALF * P, (i + 1) * HALF * P)
                        copy(sc_row[:, half], bank[6][0:SC, :], sc_f32.sem)
                        copy(sc_hl[0:SC, half], bank[6][0:SC, :], sc_hi.sem)
                for i, (o, a, k) in enumerate(((key_w[:, 0], dn, 1.0), (key_w[:, 1], dn, SLOPE),
                                               (qry_w[:, 0], ts_lo, 1.0 - SLOPE),
                                               (qry_w[:, 1], ts_hi, SLOPE - 1.0))):
                    weights_in.wait(act, b, 4)
                    act.activation(o, a[:], ACT.Exp, scale=k).then_inc(weights.sem, 1)
                value_p0(b, 0)
                value_p1(b, 0)
                for h in range(H):
                    sb_ps.wait(act, b, h + 1)
                    if h >= 1:
                        stepped.wait(act, b, h * T)
                    copy(s_bc[:], pair[:], sb_sb.sem)
                    sb_sb.wait(act, b, h + 1)
                    for jt in range(T):
                        g = h * T + jt
                        if g >= STEP_SLOTS:
                            mask1.wait(act, b, g - STEP_SLOTS + 1)
                        act.activation(step[:, g % STEP_SLOTS], s_bc[:], ACT.Relu, scale=STEP,
                                       bias=n_step[:, jt, h:h + 1]).then_inc(stepped.sem, 1)
                        if jt == 2 and h >= 1:
                            low_sums(b, h - 1)
                        if jt == 2 and h + 1 < H:
                            value_p0(b, h + 1)
                        if jt == 5 and h + 1 < H:
                            value_p1(b, h + 1)
                low_sums(b, H - 1)
                ln0_ve.wait(act, b, 1)
                act.activation(sd[:], ve[:], ACT.Sqrt).then_inc(ln0_sd.sem, 1)
                for t in range(T):
                    x1_ok.wait(act, b, t + 1)
                    copy(x1h[:, t, :], xs[:, t, :], x1_hi.sem, X1_SCALE)
                for t in range(T):
                    if t == 0:
                        rdeg_ok.wait(act, b, 1)
                    agg_ps.wait(act, b, t + 1)
                    copy(agg[:, t % 2], bank[t % 2][:], agg_sb.sem, rdeg[:, t:t + 1])
                    x1t_ps.wait(act, b, t + 1)
                    if t >= 2:
                        o_ps.wait(act, b, t - 1)
                    copy(trh[:, :, col(t % 2)], bank[2][:].rearrange("p (k n) -> p k n", k=KC), x1t_hi.sem)
                    aggt_ps.wait(act, b, t + 1)
                    copy(trh[:, :, col(2 + t % 2)], bank[3][:].rearrange("p (k n) -> p k n", k=KC), aggt_hi.sem)
                    if t >= 1:
                        ln1_ve.wait(act, b, t)
                        act.activation(sd1[:, (t - 1) % 2:(t - 1) % 2 + 1], ve1[:, (t - 1) % 2:(t - 1) % 2 + 1],
                                       ACT.Sqrt).then_inc(ln1_sd.sem, 1)
                ln1_ve.wait(act, b, T)
                act.activation(sd1[:, (T - 1) % 2:(T - 1) % 2 + 1], ve1[:, (T - 1) % 2:(T - 1) % 2 + 1],
                               ACT.Sqrt).then_inc(ln1_sd.sem, 1)

        @block.vector
        def _(dve):
            dve.wait_ge(w_in[0], 16 * KC)
            dve.tensor_copy(w0h[:], w_raw).then_inc(w_ready, 1)
            dve.wait_ge(w_ready, 1)
            dve.tensor_tensor(w0l[:], w_raw, w0h[:].bitcast(F32), ALU.subtract).then_inc(w_ready, 1)
            dve.wait_ge(w_in[1], 32)
            dve.wait_ge(consts, N_CONST)
            n = 0
            for c in range(KC):
                for k in range(2):
                    dve.tensor_tensor(prod[:, 0], w_raw[:, c, :], a_bc[:, k, :], ALU.mult).then_inc(wa_step, 1)
                    dve.wait_ge(wa_step, n + 1)
                    dve.tensor_reduce(wa32[:, c, k * H:(k + 1) * H], prod[:, 0].rearrange("p (h u) -> p h u", h=H),
                                      AX.X, ALU.add).then_inc(wa_step, 1)
                    dve.wait_ge(wa_step, n + 2)
                    n += 2
            dve.tensor_copy(wah[:, :, 0:SC], wa32[:]).then_inc(w_ready, 1)
            dve.wait_ge(w_ready, 3)
            dve.tensor_tensor(wal[:, :, 0:SC], wa32[:], wah[:, :, 0:SC].bitcast(F32),
                              ALU.subtract).then_inc(w_ready, 1)
            for c in range(2 * KC):
                dve.wait_ge(w1_hi, c + 1)
                dve.tensor_tensor(w1l[:, c, :], bank[c % 2][:], w1h[:, c, :].bitcast(F32),
                                  ALU.subtract).then_inc(w1_lo, 1)

            def value_f32(b, h):
                if h >= 1:
                    val_rest.wait(dve, b, h)
                for k in range(2):
                    dve.tensor_tensor(val32[:, k], feat[:, :, h, :],
                                      key_w[:, k, :, h:h + 1].to_broadcast([P, T, U1]),
                                      ALU.mult).then_inc(val_f32.sem, 1)

            def value_p2(b, h):
                val_p1.wait(dve, b, h + 1)
                dve.tensor_tensor(val[:, h % 2, 2], rest, val[:, h % 2, 1], ALU.subtract).then_inc(val_p2.sem, 1)

            def head_sums(b, h):
                for k in range(GROUPS):
                    low_ok.wait(dve, b, h * GROUPS + k + 1)
                    for i, q in enumerate(range(k * QPB, min(T, (k + 1) * QPB))):
                        at = i * 2 * U1
                        ins = dve.scalar_tensor_tensor(
                            out=feat[:, q, h, :], in0=bank[3 * (h % 2) + k][:, at:at + U1],
                            scalar=qry_w[:, 0, q, h:h + 1], in1=low_sum[:, h % 2, q, :],
                            op0=ALU.mult, op1=ALU.add)
                    ins.then_inc(head_ok.sem, 1)

            with dve.Fori(0, B) as b:
                steps = [0]

                def link(ins):
                    ins.then_inc(chain.sem, 1)
                    steps[0] += 1

                def linked():
                    chain.wait(dve, b, steps[0])

                link(dve.memset(feat[:, :, :, U:U1], 1.0))
                for t in range(T):
                    xt_hi.wait(dve, b, t + 1)
                    if t == HALF:
                        sc_ps.wait(dve, b, 1)
                    c = t % HALF
                    dve.tensor_tensor(trl[:, :, col(c)], bank[t % 2][:].rearrange("p (k n) -> p k n", k=KC),
                                      trh[:, :, col(c)].bitcast(F32), ALU.subtract).then_inc(xt_lo.sem, 1)
                    at_ps.wait(dve, b, 2 * t + 2)
                    dve.tensor_copy(adj_t[:, TPB:T, col(t)],
                                    bank[3][:].rearrange("p (k n) -> p k n", k=TPB)).then_inc(at_dve.sem, 1)
                    if t == HALF or t == T - 1:
                        i = 0 if t == HALF else 1
                        half = slice(i * HALF * P, (i + 1) * HALF * P)
                        sc_hi.wait(dve, b, i + 1)
                        dve.tensor_tensor(sc_hl[32:32 + SC, half], bank[6][0:SC, :],
                                          sc_hl[0:SC, half].bitcast(F32), ALU.subtract).then_inc(sc_lo.sem, 1)
                sc_f32.wait(dve, b, 2)
                link(dve.tensor_reduce(nmax16[:], sc_row[:], AX.X, ALU.max))
                linked()
                dve.tensor_scalar(diag16[:], ident[0:SC, 0:SC], nmax16[:, 0:1], None,
                                  ALU.mult).then_inc(diag_ok.sem, 1)
                nat_ps.wait(dve, b, 1)
                dve.tensor_copy(sc_nat[:], bank[7][:, 0:T * SC].rearrange("p (t s) -> p t s", t=T)).then_inc(
                    nat_sb.sem, 1)
                nat_sb.wait(dve, b, 1)
                max_ps.wait(dve, b, 1)
                link(dve.tensor_copy(nmax[:], bank[6][:, 0:SC]))
                linked()
                n_of = nmax[:, H:SC].unsqueeze(1).broadcast_to([P, T, H])
                dve.tensor_tensor(dn[:], sc_nat[:, :, H:SC], n_of, ALU.subtract).then_inc(weights_in.sem, 1)
                link(dve.tensor_tensor(ts[:], sc_nat[:, :, 0:H], n_of, ALU.add))
                dve.tensor_scalar(n_step[:], sc_nat[:, :, H:SC], STEP, None, ALU.mult).then_inc(weights_in.sem, 1)
                linked()
                dve.tensor_scalar(ts_lo[:], ts[:], 0.0, None, ALU.min).then_inc(weights_in.sem, 1)
                dve.tensor_scalar(ts_hi[:], ts[:], 0.0, None, ALU.max).then_inc(weights_in.sem, 1)
                ft_sb.wait(dve, b, T)
                weights.wait(dve, b, 4)
                value_f32(b, 0)
                value_p2(b, 0)
                at_act.wait(dve, b, T)
                at_dve.wait(dve, b, T)
                for s in range(2):
                    dve.wait_ge(y_stored[s], b * (16 * T // 2) + 16)

                def mask_upper(g):
                    h, jt = divmod(g, T)
                    stepped.wait(dve, b, g + 1)
                    if g >= MASK_SLOTS:
                        h0, j0 = divmod(g - MASK_SLOTS, T)
                        if j0 == T - 1:
                            sums_ps.wait(dve, b, (h0 + 1) * GROUPS)
                        else:
                            mask_used.wait(dve, b, h0 * (T - 1) + j0 + 1)
                    dve.tensor_tensor(mask[:, 0, g % MASK_SLOTS], step[:, g % STEP_SLOTS], adj_t[:, jt, :],
                                      ALU.min).then_inc(mask1.sem, 1)

                def mask_lower(g):
                    h, jt = divmod(g, T)
                    if jt not in POOL_KEYS:
                        mask1.wait(dve, b, g + 1)
                        dve.tensor_tensor(mask[:, 1, g % MASK_SLOTS], adj_t[:, jt, :], mask[:, 0, g % MASK_SLOTS],
                                          ALU.subtract).then_inc(mask2_dve.sem, 1)

                for g in range(H * T):
                    h, jt = divmod(g, T)
                    mask_upper(g)
                    if g >= 1:
                        mask_lower(g - 1)
                    if jt == 0 and h + 1 < H:
                        value_f32(b, h + 1)
                    if jt == 3 and h >= 1:
                        head_sums(b, h - 1)
                    if jt == 6 and h + 1 < H:
                        value_p2(b, h + 1)
                mask_lower(H * T - 1)
                head_sums(b, H - 1)
                head_ok.wait(dve, b, H * GROUPS)
                link(dve.reciprocal(rden[:].unsqueeze(3), feat[:, :, :, U:U1]))
                linked()

                def ln0_norm(t):
                    if t >= 2:
                        ln0_sum.wait(dve, b, t - 1)
                    dve.tensor_tensor(z[:, t % 2].rearrange("p (h u) -> p h u", h=H), feat[:, t, :, 0:U],
                                      rden[:, t, :].unsqueeze(2).broadcast_to([P, H, U]),
                                      ALU.mult).then_inc(ln0_att.sem, 1)

                ln0_norm(0)
                ln0_norm(1)
                for t in range(T):
                    ln0_bias.wait(dve, b, t + 1)
                    dve.scalar_tensor_tensor(out=xs[:, t, :], in0=z[:, t % 2], scalar=0.0, in1=xs[:, t, :],
                                             op0=ALU.max, op1=ALU.add).then_inc(ln0_sum.sem, 1)
                    if t + 2 < T:
                        ln0_norm(t + 2)
                    ln0_sum.wait(dve, b, t + 1)
                    link(dve.bn_stats(stats[:, t % 2], xs[:, t, :]))
                    linked()
                    stand(dve)
                    dve.bn_aggr(mv[:, t, :], stats[:, t % 2]).then_inc(ln0_mv.sem, 1)
                ln0_mv.wait(dve, b, T)
                dve.tensor_scalar(ve[:].unsqueeze(2), mv[:, :, 1:2], LN_EPS, None, ALU.add).then_inc(ln0_ve.sem, 1)
                deg_ps.wait(dve, b, 1)
                dve.tensor_scalar(degc[:], bank[7][:, 0:T], DEG_EPS, X1_SCALE, ALU.max, ALU.mult).then_inc(
                    deg_max.sem, 1)
                deg_max.wait(dve, b, 1)
                dve.reciprocal(rdeg[:], degc[:]).then_inc(rdeg_ok.sem, 1)
                ln0_sd.wait(dve, b, 1)
                link(dve.reciprocal(rs[:], sd[:]))
                linked()
                for t in range(T):
                    dve.tensor_scalar(xs[:, t, :], xs[:, t, :], mv[:, t, 0:1], rs[:, t:t + 1],
                                      ALU.subtract, ALU.mult).then_inc(x1_ok.sem, 1)
                    if t >= 1:
                        x1_hi.wait(dve, b, t)
                        dve.scalar_tensor_tensor(out=x1l[:, t - 1, :], in0=xs[:, t - 1, :], scalar=X1_SCALE,
                                                 in1=x1h[:, t - 1, :], op0=ALU.mult,
                                                 op1=ALU.subtract).then_inc(x1_lo.sem, 1)
                x1_hi.wait(dve, b, T)
                dve.scalar_tensor_tensor(out=x1l[:, T - 1, :], in0=xs[:, T - 1, :], scalar=X1_SCALE,
                                         in1=x1h[:, T - 1, :], op0=ALU.mult,
                                         op1=ALU.subtract).then_inc(x1_lo.sem, 1)

                def ln1(t):
                    s = t % 2
                    if t >= 2:
                        y_ok.wait(dve, b, t - 1)
                    o_ps.wait(dve, b, t + 1)
                    dve.scalar_tensor_tensor(out=z[:, s], in0=bank[4 + s][:], scalar=0.0, in1=xs[:, t, :],
                                             op0=ALU.max, op1=ALU.add).then_inc(res_ok.sem, 1)
                    res_ok.wait(dve, b, t + 1)
                    link(dve.bn_stats(stats[:, s], z[:, s]))
                    linked()
                    stand(dve)
                    link(dve.bn_aggr(mv1[:, s], stats[:, s]))
                    linked()
                    dve.tensor_scalar(ve1[:, s:s + 1], mv1[:, s, 1:2], LN_EPS, None, ALU.add).then_inc(ln1_ve.sem, 1)

                def ln1_end(t):
                    s = t % 2
                    ln1_sd.wait(dve, b, t + 1)
                    link(dve.reciprocal(rs1[:, s:s + 1], sd1[:, s:s + 1]))
                    linked()
                    dve.wait_ge(y_stored[s], b * (16 * T // 2) + 16 * (t // 2) + 16)
                    dve.tensor_scalar(y_out[:, s], z[:, s], mv1[:, s, 0:1], rs1[:, s:s + 1],
                                      ALU.subtract, ALU.mult).then_inc(y_ok.sem, 1)

                for t in range(T):
                    x1t_hi.wait(dve, b, t + 1)
                    dve.tensor_tensor(trl[:, :, col(t % 2)], bank[2][:].rearrange("p (k n) -> p k n", k=KC),
                                      trh[:, :, col(t % 2)].bitcast(F32), ALU.subtract).then_inc(x1t_lo.sem, 1)
                    aggt_hi.wait(dve, b, t + 1)
                    dve.tensor_tensor(trl[:, :, col(2 + t % 2)], bank[3][:].rearrange("p (k n) -> p k n", k=KC),
                                      trh[:, :, col(2 + t % 2)].bitcast(F32), ALU.subtract).then_inc(aggt_lo.sem, 1)
                    if t >= 1:
                        ln1(t - 1)
                    if t >= 2:
                        ln1_end(t - 2)
                ln1(T - 1)
                ln1_end(T - 2)
                ln1_end(T - 1)
                assert steps[0] == chain.per_batch, steps

        @block.tensor
        def _(pe):
            def mm(o, l, r, start, stop):
                return pe.matmul(o, l, r, start=start, stop=stop, skip_group_check=True)

            pe.wait_ge(consts, 1)
            pe.wait_ge(w_in[3], 16)
            for f in range(2 * KC):
                if f >= 2:
                    pe.wait_ge(w1_lo, f - 1)
                for c in range(KC):
                    ins = pe.transpose(bank[f % 2][:, col(c)], sage_raw[:, c, f * P:(f + 1) * P], ident[:])
                ins.then_inc(w1_ps, 1)
            pe.wait_ge(w1_lo, 2 * KC)
            pe.wait_ge(w_ready, 4)
            pe.wait_ge(consts, N_CONST)

            def split_product(o, lh, ll, rh, rl, first=True, last=True):
                n = len(lh)
                for k in range(n):
                    for i, (a, c) in enumerate(((lh[k], rh[k]), (lh[k], rl[k]), (ll[k], rh[k]))):
                        ins = mm(o, a, c, first and k == 0 and i == 0, last and k == n - 1 and i == 2)
                return ins

            with pe.Fori(0, B) as b:
                def features(t):
                    c = t % HALF
                    xt_hi.wait(pe, b, t + 1)
                    xt_lo.wait(pe, b, t + 1)
                    if t >= 2:
                        ft_sb.wait(pe, b, t - 1)
                    split_product(bank[4 + t % 2][:], [trh[:, k, col(c)] for k in range(KC)],
                                  [trl[:, k, col(c)] for k in range(KC)], [w0h[:, k, :] for k in range(KC)],
                                  [w0l[:, k, :] for k in range(KC)]).then_inc(ft_ps.sem, 1)

                def scores(i):
                    if i == 1:
                        sc_f32.wait(pe, b, 1)
                        sc_lo.wait(pe, b, 1)
                    split_product(bank[6][:], [wah[:, k, :] for k in range(KC)], [wal[:, k, :] for k in range(KC)],
                                  [trh[:, k, :] for k in range(KC)],
                                  [trl[:, k, :] for k in range(KC)]).then_inc(sc_ps.sem, 1)

                for t in range(T):
                    x_in[t].wait(pe, b, 16)
                    if t >= 2:
                        xt_lo.wait(pe, b, t - 1)
                    for k in range(KC):
                        ins = pe.transpose(bank[t % 2][:, col(k)], xs[:, t, col(k)], ident[:])
                    ins.then_inc(xt_ps.sem, 1)
                    pe.wait_ge(a_in[t % 2], b * (16 * T // 2) + 16 * (t // 2) + 16)
                    for half, done in ((0, at_act), (1, at_dve)):
                        if t >= 1:
                            done.wait(pe, b, t)
                        for k in range(TPB):
                            jt = half * TPB + k
                            ins = pe.transpose(bank[2 + half][:, col(k)], adj_nat[:, t % 2, col(jt)], ident[:])
                        ins.then_inc(at_ps.sem, 1)
                    if t >= 1:
                        features(t - 1)
                    if t == HALF:
                        scores(0)
                features(T - 1)
                scores(1)
                sc_f32.wait(pe, b, 2)
                stand(pe)
                for t in range(T):
                    ins = pe.transpose(bank[7][:, t * SC:(t + 1) * SC], sc_row[:, col(t)], ident[0:SC, 0:SC])
                ins.then_inc(nat_ps.sem, 1)
                diag_ok.wait(pe, b, 1)
                sc_lo.wait(pe, b, 2)
                mm(bank[6][:, 0:SC], ones16[:], diag16[:], True, True).then_inc(max_ps.sem, 1)

                def broadcast(h):
                    if h == 0:
                        nat_sb.wait(pe, b, 1)
                        weights_in.wait(pe, b, 4)
                    else:
                        sb_sb.wait(pe, b, h)
                    for i in range(2):
                        ins = mm(bank[6 + i], pick[:, h, :], sc_hl[:, i * BANK:(i + 1) * BANK], True, True)
                    ins.then_inc(sb_ps.sem, 1)

                broadcast(0)
                for h in range(H):
                    val_p2.wait(pe, b, h + 1)
                    if h >= 2:
                        head_ok.wait(pe, b, (h - 1) * GROUPS)
                    for jt in range(T):
                        g = h * T + jt
                        if jt in POOL_KEYS:
                            mask2_pool.wait(pe, b, h * NPOOL + POOL_KEYS.index(jt) + 1)
                        else:
                            mask2_dve.wait(pe, b, h * NDVE + jt - sum(k < jt for k in POOL_KEYS) + 1)
                        mask1.wait(pe, b, g + 1)
                        for q in range(T):
                            k, i = divmod(q, QPB)
                            for kind in range(2):
                                at = (2 * i + kind) * U1
                                for part in range(PARTS):
                                    ins = mm(bank[3 * (h % 2) + k][:, at:at + U1],
                                             mask[:, kind, g % MASK_SLOTS, col(q)],
                                             val[:, h % 2, part, kind, jt, :],
                                             jt == 0 and i == 0 and kind == 0 and part == 0,
                                             jt == T - 1)
                            if jt == T - 1 and (i == QPB - 1 or q == T - 1):
                                if q < T - 1:
                                    ins.then_inc(sums_ps.sem, 1)
                        if jt < T - 1:
                            ins.then_inc(mask_used.sem, 1)
                        else:
                            ins.then_inc(sums_ps.sem, 1)
                        if jt == 1 and h + 1 < H:
                            broadcast(h + 1)
                for q in range(T):
                    for jt in range(T):
                        ins = mm(bank[7][:, q:q + 1], adj_t[:, jt, col(q)], ones_bf[:], jt == 0, jt == T - 1)
                ins.then_inc(deg_ps.sem, 1)

                def aggregate(t):
                    if t >= 2:
                        agg_sb.wait(pe, b, t - 1)
                    for jt in range(T):
                        for i, r in enumerate((x1h, x1l)):
                            ins = mm(bank[t % 2][:], adj_t[:, jt, col(t)], r[:, jt, :], jt == 0 and i == 0,
                                     jt == T - 1 and i == 1)
                    ins.then_inc(agg_ps.sem, 1)
                    if t >= 1:
                        x1t_lo.wait(pe, b, t)
                    for k in range(KC):
                        ins = pe.transpose(bank[2][:, col(k)], xs[:, t, col(k)], ident[:])
                    ins.then_inc(x1t_ps.sem, 1)

                x1_lo.wait(pe, b, T)
                head_ok.wait(pe, b, H * GROUPS)
                aggregate(0)
                for t in range(T):
                    if t + 1 < T:
                        aggregate(t + 1)
                    agg_sb.wait(pe, b, t + 1)
                    if t >= 1:
                        aggt_lo.wait(pe, b, t)
                    for k in range(KC):
                        ins = pe.transpose(bank[3][:, col(k)], agg[:, t % 2, col(k)], ident[:])
                    ins.then_inc(aggt_ps.sem, 1)
                    x1t_lo.wait(pe, b, t + 1)
                    if t >= 2:
                        res_ok.wait(pe, b, t - 1)
                    xs_t = [(tr[:, k, col(t % 2)]) for tr in (trh, trl) for k in range(KC)]
                    ag_t = [(tr[:, k, col(2 + t % 2)]) for tr in (trh, trl) for k in range(KC)]
                    split_product(bank[4 + t % 2][:], xs_t[:KC], xs_t[KC:], [w1h[:, k, :] for k in range(KC)],
                                  [w1l[:, k, :] for k in range(KC)], last=False)
                    aggt_hi.wait(pe, b, t + 1)
                    aggt_lo.wait(pe, b, t + 1)
                    split_product(bank[4 + t % 2][:], ag_t[:KC], ag_t[KC:], [w1h[:, KC + k, :] for k in range(KC)],
                                  [w1l[:, KC + k, :] for k in range(KC)], first=False).then_inc(o_ps.sem, 1)
                res_ok.wait(pe, b, T)


_INS = ["x", "adj", "L0_gnn_W", "L0_gnn_b", "L0_gnn_a_self", "L0_gnn_a_neigh", "L1_gnn_W"]


def kernel(**inputs):
    import numpy as _np
    import concourse.bacc as _bacc
    from concourse import mybir as _mybir
    from concourse.bass_utils import run_bass_kernel_spmd as _run

    nc = _bacc.Bacc("TRN2", target_bir_lowering=False, num_devices=1)
    arrays, args = {}, []
    for name in _INS:
        a = _np.ascontiguousarray(inputs[name])
        arrays[f"in_{name}_dram"] = a
        args.append(nc.dram_tensor(f"in_{name}_dram", a.shape, _mybir.dt.from_np(a.dtype), kind="ExternalInput").ap())
    out = nc.dram_tensor("out_0_dram", inputs["x"].shape, _mybir.dt.float32, kind="ExternalOutput").ap()
    gat_sage_kernel(nc, *args, out)
    r = _run(nc, [arrays], core_ids=[0])
    return r.results[0]["out_0_dram"]
```

```python
from contextlib import ExitStack

import concourse.bass as bass
from concourse import mybir

F32 = mybir.dt.float32
F32R = mybir.dt.float32r
BF16 = mybir.dt.bfloat16
F16 = mybir.dt.float16
ALU = mybir.AluOpType
ACT = mybir.ActivationFunctionType
AX = mybir.AxisListType

P = 128
LN_EPS = 1e-5
DEG_EPS = 1e-6
SLOPE = 0.2
STEP = 2.0 ** 100
X1_SCALE = 2.0 ** 11
MASK_SLOTS = 6
STEP_SLOTS = 3
PARTS = 3


class Signal:

    def __init__(self, sem, per_batch):
        self.sem, self.per_batch = sem, per_batch

    def wait(self, engine, batch, count):
        assert 0 < count <= self.per_batch
        engine.wait_ge(self.sem, batch * self.per_batch + count)


def gat_sage_kernel(nc, x, adj, gat_w, gat_b, gat_self, gat_neigh, sage_w, out):
    B, N, D = x.shape
    H, _, U = gat_w.shape
    T = N // P
    KC = D // P
    HALF = T // 2
    U1 = U + 1
    HU = H * U
    SC = 2 * H
    BANK = 512
    TPB = BANK // P
    QPB = 3
    GROUPS = (T + QPB - 1) // QPB
    lower_by, made = {}, [0, 0]
    for h in range(H):
        for jt in range(T):
            by_pool = jt in (1, 4) or (jt == 6 and h < H - 1)
            made[by_pool] += 1
            lower_by[h, jt] = by_pool, made[by_pool]
    NDVE, NPOOL = made
    AGG_BANKS = ((0, 1, 2, 6), (7, 3, 0, 1))
    O1_BANKS = (4, 6)
    FIRST, SECOND = slice(0, HALF), slice(HALF, T)
    CHAIN = 5 + 4 * T

    with ExitStack() as ctx:
        def sb(name, shape, dt):
            return ctx.enter_context(nc.sbuf_tensor(name, shape, dt))

        def sem(name):
            return ctx.enter_context(nc.semaphore(name))

        ident = sb("ident", [P, P], F32)
        ident_bf = sb("ident_bf", [P, P], BF16)
        ones_bf = sb("ones_bf", [P, 1], BF16)
        ones16 = sb("ones16", [SC, P], F32)
        pick = sb("pick", [48, H], F32R)
        bias_bc = sb("bias_bc", [P, HU], F32)
        w0h = sb("w0h", [P, KC, HU], F32R)
        w0l = sb("w0l", [P, KC, HU], F32R)
        wah_wide = sb("wah_wide", [P, (KC - 1) * SC + P], F32R)
        wal_wide = sb("wal_wide", [P, (KC - 1) * SC + P], F32R)
        wah, wal = (w[:, 0:KC * SC].rearrange("p (c n) -> p c n", c=KC) for w in (wah_wide, wal_wide))
        w1h = sb("w1h", [P, 2 * KC, D], F32R)
        w1l = sb("w1l", [P, 2 * KC, D], F32R)
        xs = sb("xs", [P, T, D], F32)
        x1_parts = sb("x1_parts", [P, 2, T, D], F16)
        x1h, x1l = x1_parts[:, 0], x1_parts[:, 1]
        pool32 = x1_parts[:, :, :, :].rearrange("p k t d -> p (k t d)").bitcast(F32)

        def head_buffer(k):
            return pool32[:, k * 2 * T * U1:(k + 1) * 2 * T * U1].rearrange("p (k t u) -> p k t u", k=2, t=T)

        val32 = head_buffer(0)
        weighted = head_buffer(1).rearrange("p k t u -> p (k t u)").rearrange("p (t k u) -> p t k u", k=2, u=U1)
        feat = sb("feat", [P, T, H, U1], F32)
        trh = sb("trh", [P, KC, HALF * P], F32R)
        trl = sb("trl", [P, KC, HALF * P], F32R)
        adj_nat = sb("adj_nat", [P, 2, N], F32)
        adj_bf = sb("adj_bf", [P, 2, N], BF16)
        adj_t = sb("adj_t", [P, T, N], BF16)
        sc_row = sb("sc_row", [SC, N], F32)
        sc_hl = sb("sc_hl", [48, N], F32R)
        s_bc = sb("s_bc", [P, N], F32)
        x1t_h = sb("x1t_h", [P, KC, P], F32R)
        x1t_l = sb("x1t_l", [P, KC, P], F32R)
        step = sb("step", [P, STEP_SLOTS, N], BF16)
        mask = sb("mask", [P, 2, MASK_SLOTS, N], BF16)
        val = sb("val", [P, 2, PARTS, 2, T, U1], BF16)
        sc_nat = sb("sc_nat", [P, T, SC], F32)
        nmax16 = sb("nmax16", [SC, 1], F32)
        diag16 = sb("diag16", [SC, SC], F32)
        nmax = sb("nmax", [P, SC], F32)
        n_step = sb("n_step", [P, T, H], F32)
        dn = sb("dn", [P, T, H], F32)
        ts = sb("ts", [P, T, H], F32)
        ts_lo = sb("ts_lo", [P, T, H], F32)
        ts_hi = sb("ts_hi", [P, T, H], F32)
        key_w = sb("key_w", [P, 2, T, H], F32)
        qry_w = sb("qry_w", [P, 2, T, H], F32)
        rden = sb("rden", [P, T, H], F32)
        z = s_bc[:, :].rearrange("p (s d) -> p s d", s=2)
        stats = sb("stats", [P, 2, 6], F32)
        mv = sb("mv", [P, T, 2], F32)
        sd = sb("sd", [P, T], F32)
        rs = sb("rs", [P, T], F32)
        mv1 = sb("mv1", [P, 2, 2], F32)
        sd1 = sb("sd1", [P, 2], F32)
        rs1 = sb("rs1", [P, 2], F32)
        degc = sb("degc", [P, T], F32)
        eps = sb("eps", [P, 2], F32)
        nb = sb("nb", [P, T], F32)
        rdeg = sb("rdeg", [P, T], F32)
        mask32 = mask[:, :, :, :].rearrange("p k s n -> p (k s n)").bitcast(F32)
        o2s = mask32[:, 0:2 * D].rearrange("p (s d) -> p s d", s=2)
        y_out = mask32[:, 2 * D:4 * D].rearrange("p (s d) -> p s d", s=2)
        w_raw = feat[:, 0:4, :, :].rearrange("p a b c -> p (a b c)")[:, 0:KC * HU].rearrange(
            "p (c n) -> p c n", c=KC)
        a_bc = z
        prod = y_out
        wa32 = sb("wa32", [P, KC, SC], F32)
        sage_raw = xs[:, :, :].rearrange("p t d -> p (t d)").rearrange("p (c f) -> p c f", c=KC)
        pick32 = o2s[0:48, 0, 0:H]

        bank = [ctx.enter_context(nc.psum_tensor(f"bank{k}", [P, BANK], F32)) for k in range(6)]
        pair = ctx.enter_context(nc.psum_tensor("pair", [P, 2 * BANK], F32))
        bank += [pair[:, 0:BANK], pair[:, BANK:2 * BANK]]

        w_in = [sem(f"w_in{k}") for k in range(4)]
        pool_const, consts = sem("pool_const"), sem("consts")
        w_ready, w1_ps, w1_hi, w1_lo, wa_step = (
            sem("w_ready"), sem("w1_ps"), sem("w1_hi"), sem("w1_lo"), sem("wa_step"))
        x_in = [Signal(sem(f"x_in{t}"), 16) for t in range(T)]
        a_in = [sem(f"a_in{s}") for s in range(2)]
        y_stored = [sem(f"y_stored{s}") for s in range(2)]

        def signal(name, per_batch):
            return Signal(sem(name), per_batch)

        xt_ps = signal("xt_ps", T)
        xt_hi = signal("xt_hi", T)
        xt_lo = signal("xt_lo", T)
        adj_cast = signal("adj_cast", T)
        at_ps = signal("at_ps", T)
        at_sb = signal("at_sb", T)
        ft_ps = signal("ft_ps", T)
        ft_sb = signal("ft_sb", T)
        sc_ps = signal("sc_ps", 2)
        sc_f32 = signal("sc_f32", 2)
        sc_hi = signal("sc_hi", 2)
        sc_lo = signal("sc_lo", 2)
        nat_ps = signal("nat_ps", 1)
        nat_sb = signal("nat_sb", 1)
        diag_ok = signal("diag_ok", 1)
        max_ps = signal("max_ps", 1)
        weights_in = signal("weights_in", 4)
        weights = signal("weights", 4)
        chain = signal("chain", CHAIN)
        sb_ps = signal("sb_ps", H)
        sb_sb = signal("sb_sb", H)
        stepped = signal("stepped", H * T)
        mask1 = signal("mask1", H * T)
        mask2_dve = signal("mask2_dve", NDVE)
        mask2_pool = signal("mask2_pool", NPOOL)
        mask_used = signal("mask_used", H * (T - 1))
        val_f32 = signal("val_f32", 2 * H)
        val_p0 = signal("val_p0", H + 1)
        val_rest0 = signal("val_rest0", 2)
        val_rest = signal("val_rest", H - 1)
        val_p1 = signal("val_p1", H + 1)
        val_p2 = signal("val_p2", H + 1)
        sums_ps = signal("sums_ps", H * GROUPS)
        weighted_ok = signal("weighted_ok", H * GROUPS)
        head_ok = signal("head_ok", H - 1)
        last_head_ok = signal("last_head_ok", 1)
        deg_ps = signal("deg_ps", 1)
        deg_max = signal("deg_max", 1)
        rdeg_ok = signal("rdeg_ok", 1)
        rden_ok = signal("rden_ok", 1)
        ln0_norm = signal("ln0_norm", T)
        ln0_sum = signal("ln0_sum", T)
        ln0_mv = signal("ln0_mv", T)
        ln0_sd = signal("ln0_sd", T)
        ln0_nb = signal("ln0_nb", T)
        x1_ok = signal("x1_ok", T)
        x1_hi = signal("x1_hi", T)
        x1_lo = signal("x1_lo", T)
        agg_ps = signal("agg_ps", 2 * KC)
        aggt_hi = signal("aggt_hi", 2 * KC)
        aggt_lo = signal("aggt_lo", 2 * KC)
        x1t_ps = signal("x1t_ps", T)
        x1t_hi = signal("x1t_hi", T)
        x1t_lo = signal("x1t_lo", T)
        o1_ps = signal("o1_ps", T)
        o2_ps = signal("o2_ps", T)
        o2_sb = signal("o2_sb", T)
        o_sum = signal("o_sum", T)
        res_ok = signal("res_ok", T)
        ln1_mv = signal("ln1_mv", T)
        ln1_sd = signal("ln1_sd", T)
        y_ok = signal("y_ok", T)

        def rows(v):
            return v.rearrange("h u -> (h u)").partition_broadcast(P)

        def col(c):
            return slice(c * P, (c + 1) * P)

        N_CONST = 10
        turnstile = sem("turnstile")

        def stand(engine):
            engine.sem_inc(turnstile, 1)

        block = ctx.enter_context(nc.Block())

        @block.sync
        def _(sp):
            for c in range(KC):
                sp.dma_start(w_raw[:, c, :].rearrange("p (h u) -> p h u", h=H),
                             gat_w[:, col(c), :].rearrange("h p u -> p h u")).then_inc(w_in[0], 16)
            sp.dma_start(a_bc[:, 0, :], rows(gat_self)).then_inc(w_in[1], 16)
            sp.dma_start(a_bc[:, 1, :], rows(gat_neigh)).then_inc(w_in[1], 16)
            sp.dma_start(bias_bc[:, :], rows(gat_b)).then_inc(w_in[2], 16)
            sp.dma_start(sage_raw, sage_w.rearrange("(c p) f -> p c f", p=P)).then_inc(w_in[3], 16)
            sp.sem_inc(y_stored[0], 16)
            sp.sem_inc(y_stored[1], 16)

            def load_x(b, t):
                sp.dma_start(xs[:, t, :], x[b, t * P:(t + 1) * P, :]).then_inc(x_in[t].sem, 16)

            def load_adj(b, t):
                sp.dma_start(adj_nat[:, t % 2, :], adj[b, t * P:(t + 1) * P, :]).then_inc(a_in[t % 2], 16)

            def store_y(b, t):
                y_ok.wait(sp, b, t + 1)
                sp.dma_start(out[b, t * P:(t + 1) * P, :], y_out[:, t % 2, :]).then_inc(y_stored[t % 2], 16)

            def load_late_adj(b):
                for t in range(2, T):
                    adj_cast.wait(sp, b, t - 1)
                    load_adj(b, t)

            for t in range(2):
                load_adj(0, t)
            sp.wait_ge(w1_ps, 2 * KC)
            for t in range(T):
                load_x(0, t)
            load_late_adj(0)
            with sp.Fori(0, B - 1) as b:
                for t in range(2):
                    adj_cast.wait(sp, b, T - 1 + t)
                    load_adj(b + 1, t)
                for t in range(T):
                    res_ok.wait(sp, b, t + 1)
                    load_x(b + 1, t)
                    store_y(b, t)
                load_late_adj(b + 1)
            for t in range(T):
                store_y(B - 1, t)
            for s in range(2):
                sp.wait_ge(y_stored[s], 16 * (B * T // 2 + 1))

        @block.gpsimd
        def _(pool):
            pool.memset(ident[:], 0.0).then_inc(pool_const, 1)
            pool.memset(pick32, 0.0).then_inc(pool_const, 1)
            pool.wait_ge(pool_const, 2)
            pool.affine_select(out=ident[:], in_=ident[:], compare_op=ALU.not_equal, fill=1.0, base=0,
                               pattern=[[-1, P]], channel_multiplier=1).then_inc(consts, 1)
            for base in (0, -32):
                pool.affine_select(out=pick32, in_=pick32, compare_op=ALU.not_equal, fill=1.0,
                                   base=base, pattern=[[-1, H]],
                                   channel_multiplier=1).then_inc(pool_const, 1)
                pool.wait_ge(pool_const, 3 if base == 0 else 4)
            pool.tensor_copy(pick[:], pick32).then_inc(consts, 1)
            pool.wait_ge(consts, 1)
            pool.tensor_copy(ident_bf[:], ident[:]).then_inc(consts, 1)
            pool.memset(ones16[:], 1.0).then_inc(consts, 1)
            pool.memset(ones_bf[:], 1.0).then_inc(consts, 1)
            pool.memset(eps[:, 0:1], LN_EPS / X1_SCALE ** 2).then_inc(consts, 1)
            pool.memset(eps[:, 1:2], LN_EPS * X1_SCALE ** 2).then_inc(consts, 1)
            pool.memset(sc_hl[:].bitcast(F32), 0.0).then_inc(consts, 1)
            pool.memset(wah_wide[:].bitcast(F32), 0.0).then_inc(consts, 1)
            pool.memset(wal_wide[:].bitcast(F32), 0.0).then_inc(consts, 1)

            def value_rest(b, h):
                val_f32.wait(pool, b, 2 * h + 2)
                val_p0.wait(pool, b, h + 2)
                pool.tensor_tensor(val32, val32, val[:, h % 2, 0], ALU.subtract).then_inc(val_rest.sem, 1)

            def add_branches(b, h):
                weighted_ok.wait(pool, b, (h + 1) * GROUPS)
                pool.tensor_tensor(feat[:, :, h, :], weighted[:, :, 0, :], weighted[:, :, 1, :],
                                   ALU.add).then_inc(head_ok.sem, 1)

            with pool.Fori(0, B) as b:
                for h in range(H):
                    for jt in range(T):
                        by_pool, _ = lower_by[h, jt]
                        if not by_pool:
                            continue
                        g = h * T + jt
                        mask1.wait(pool, b, g + 1)
                        pool.tensor_tensor(mask[:, 1, g % MASK_SLOTS], adj_t[:, jt, :],
                                           mask[:, 0, g % MASK_SLOTS],
                                           ALU.subtract).then_inc(mask2_pool.sem, 1)
                        if jt == 1 and h + 1 < H:
                            value_rest(b, h + 1)
                        if jt == 4 and h >= 1:
                            add_branches(b, h - 1)

                def norm(t):
                    if t >= 2:
                        ln0_sum.wait(pool, b, t - 1)
                    pool.tensor_tensor(z[:, t % 2].rearrange("p (h u) -> p h u", h=H), feat[:, t, :, 0:U],
                                       rden[:, t, :].unsqueeze(2).broadcast_to([P, H, U]),
                                       ALU.mult).then_inc(ln0_norm.sem, 1)

                def x1_low(t):
                    x1_hi.wait(pool, b, t + 1)
                    pool.tensor_tensor(x1l[:, t, :], xs[:, t, :], x1h[:, t, :], ALU.subtract).then_inc(x1_lo.sem, 1)

                rden_ok.wait(pool, b, 1)
                last_head_ok.wait(pool, b, 1)
                ln0_norm.wait(pool, b, 1)
                norm(1)
                norm(2)
                for t in range(T):
                    x1_low(t)
                    if t + 3 < T:
                        norm(t + 3)

        @block.scalar
        def _(act):
            def copy(o, i, s, scale=1.0):
                act.activation(o, i, ACT.Copy, scale=scale).then_inc(s, 1)

            for c in range(2 * KC):
                act.wait_ge(w1_ps, c + 1)
                copy(w1h[:, c, :], bank[c % 2][:], w1_hi)

            def value_p0(b, h, tiles=slice(0, T)):
                val_f32.wait(act, b, 2 * h + (1 if tiles.stop == HALF else 2))
                if h >= 2:
                    sums_ps.wait(act, b, (h - 1) * GROUPS)
                copy(val[:, h % 2, 0, :, tiles], val32[:, :, tiles], val_p0.sem)

            def value_p1(b, h, tiles=slice(0, T)):
                if h == 0:
                    val_rest0.wait(act, b, 1 if tiles.stop == HALF else 2)
                else:
                    val_rest.wait(act, b, h)
                copy(val[:, h % 2, 1, :, tiles], val32[:, :, tiles], val_p1.sem)

            with act.Fori(0, B) as b:
                def x_high(t):
                    xt_ps.wait(act, b, t + 1)
                    if t == HALF:
                        sc_ps.wait(act, b, 1)
                    if t >= HALF:
                        ft_ps.wait(act, b, t - HALF + 1)
                    copy(trh[:, :, col(t % HALF)], bank[t % 2][:].rearrange("p (k n) -> p k n", k=KC), xt_hi.sem)

                def cast_adj(t):
                    act.wait_ge(a_in[t % 2], b * (16 * T // 2) + 16 * (t // 2) + 16)
                    if t >= 2:
                        at_ps.wait(act, b, t - 1)
                    copy(adj_bf[:, t % 2], adj_nat[:, t % 2], adj_cast.sem)

                def score_rows(i):
                    sc_ps.wait(act, b, i + 1)
                    half = slice(i * HALF * P, (i + 1) * HALF * P)
                    copy(sc_row[:, half], bank[6][0:SC, :], sc_f32.sem)
                    copy(sc_hl[0:SC, half], bank[6][0:SC, :], sc_hi.sem)

                def self_scores(h):
                    sb_ps.wait(act, b, h + 1)
                    if h >= 1:
                        stepped.wait(act, b, h * T)
                    copy(s_bc[:], pair[:], sb_sb.sem)
                    sb_sb.wait(act, b, h + 1)

                def make_step(g):
                    h, jt = divmod(g, T)
                    if g >= STEP_SLOTS:
                        mask1.wait(act, b, g - STEP_SLOTS + 1)
                    act.activation(step[:, g % STEP_SLOTS], s_bc[:], ACT.Relu, scale=STEP,
                                   bias=n_step[:, jt, h:h + 1]).then_inc(stepped.sem, 1)

                def weight_exp(o, a, k):
                    weights_in.wait(act, b, 4)
                    act.activation(o, a[:], ACT.Exp, scale=k).then_inc(weights.sem, 1)

                cast_adj(0)
                cast_adj(1)
                x_high(0)
                cast_adj(2)
                x_high(1)
                x_high(2)
                cast_adj(3)
                x_high(3)
                cast_adj(4)
                x_high(4)
                x_high(5)
                score_rows(0)
                x_high(6)
                x_high(7)
                cast_adj(5)
                score_rows(1)
                cast_adj(6)
                cast_adj(7)
                weight_exp(key_w[:, 0], dn, 1.0)
                weight_exp(key_w[:, 1], dn, SLOPE)
                value_p0(b, 0, FIRST)
                weight_exp(qry_w[:, 0], ts_lo, 1.0 - SLOPE)
                weight_exp(qry_w[:, 1], ts_hi, SLOPE - 1.0)
                self_scores(0)
                value_p1(b, 0, FIRST)
                make_step(0)
                make_step(1)
                value_p0(b, 0, SECOND)
                make_step(2)
                value_p1(b, 0, SECOND)
                for h in range(H):
                    if h >= 1:
                        self_scores(h)
                    for jt in range(T):
                        g = h * T + jt
                        if g >= 3:
                            make_step(g)
                        if jt == 3 and h + 1 < H:
                            value_p0(b, h + 1)
                        if jt == 5 and h + 1 < H:
                            value_p1(b, h + 1)

                def x1_high(t):
                    ln0_nb.wait(act, b, t + 1)
                    act.activation(xs[:, t, :], xs[:, t, :], ACT.Identity, bias=nb[:, t:t + 1],
                                   scale=rs[:, t:t + 1]).then_inc(x1_ok.sem, 1)
                    x1_ok.wait(act, b, t + 1)
                    copy(x1h[:, t, :], xs[:, t, :], x1_hi.sem)

                def x1t_high(t):
                    x1t_ps.wait(act, b, t + 1)
                    if t >= 1:
                        o1_ps.wait(act, b, t)
                    copy(x1t_h[:], bank[5][:].rearrange("p (k n) -> p k n", k=KC), x1t_hi.sem)

                for t in range(T):
                    ln0_mv.wait(act, b, t + 1)
                    act.activation(sd[:, t:t + 1], mv[:, t, 1:2], ACT.Sqrt, bias=eps[:, 0:1],
                                   scale=1.0 / X1_SCALE ** 2).then_inc(ln0_sd.sem, 1)
                    x1_high(t)
                    if t == 3:
                        x1t_high(0)

                def agg_high(half):
                    for f in range(KC):
                        agg_ps.wait(act, b, half * KC + f + 1)
                        copy(trh[:, f, :], bank[AGG_BANKS[half][f]][:], aggt_hi.sem)

                def by_degree(t):
                    if t == 0:
                        rdeg_ok.wait(act, b, 1)
                    o2_ps.wait(act, b, t + 1)
                    if t >= 2:
                        o_sum.wait(act, b, t - 1)
                    copy(o2s[:, t % 2], bank[2][:], o2_sb.sem, rdeg[:, t:t + 1])

                def ln1_root(t):
                    ln1_mv.wait(act, b, t + 1)
                    act.activation(sd1[:, t % 2:t % 2 + 1], mv1[:, t % 2, 1:2], ACT.Sqrt,
                                   bias=eps[:, 1:2]).then_inc(ln1_sd.sem, 1)

                agg_high(0)
                x1t_high(1)
                for t in range(T):
                    by_degree(t)
                    if t == HALF - 1:
                        agg_high(1)
                    if t + 2 < T:
                        x1t_high(t + 2)
                    if t >= 1:
                        ln1_root(t - 1)
                ln1_root(T - 1)

        @block.vector
        def _(dve):
            dve.wait_ge(w_in[0], 16 * KC)
            dve.tensor_copy(w0h[:], w_raw).then_inc(w_ready, 1)
            dve.wait_ge(w_ready, 1)
            dve.tensor_tensor(w0l[:], w_raw, w0h[:].bitcast(F32), ALU.subtract).then_inc(w_ready, 1)
            dve.wait_ge(w_in[1], 32)
            dve.wait_ge(consts, N_CONST)
            n = 0
            for c in range(KC):
                for k in range(2):
                    dve.tensor_tensor(prod[:, 0], w_raw[:, c, :], a_bc[:, k, :], ALU.mult).then_inc(wa_step, 1)
                    dve.wait_ge(wa_step, n + 1)
                    dve.tensor_reduce(wa32[:, c, k * H:(k + 1) * H], prod[:, 0].rearrange("p (h u) -> p h u", h=H),
                                      AX.X, ALU.add).then_inc(wa_step, 1)
                    dve.wait_ge(wa_step, n + 2)
                    n += 2
            dve.tensor_copy(wah, wa32[:]).then_inc(w_ready, 1)
            dve.wait_ge(w_ready, 3)
            dve.tensor_tensor(wal, wa32[:], wah.bitcast(F32),
                              ALU.subtract).then_inc(w_ready, 1)
            for c in range(2 * KC):
                dve.wait_ge(w1_hi, c + 1)
                dve.tensor_tensor(w1l[:, c, :], bank[c % 2][:], w1h[:, c, :].bitcast(F32),
                                  ALU.subtract).then_inc(w1_lo, 1)

            def value_f32(b, h, tiles):
                if h >= 1:
                    val_p2.wait(dve, b, h + 1)
                dve.tensor_tensor(val32[:, :, tiles], feat[:, tiles, h, :].unsqueeze(1).broadcast_to([P, 2, HALF, U1]),
                                  key_w[:, :, tiles, h:h + 1].to_broadcast([P, 2, HALF, U1]),
                                  ALU.mult).then_inc(val_f32.sem, 1)

            def value_rest0(b, tiles):
                count = 1 if tiles.stop == HALF else 2
                val_p0.wait(dve, b, count)
                val_f32.wait(dve, b, count)
                dve.tensor_tensor(val32[:, :, tiles], val32[:, :, tiles], val[:, 0, 0, :, tiles],
                                  ALU.subtract).then_inc(val_rest0.sem, 1)

            def value_p2(b, h, tiles=slice(0, T)):
                if h == 0:
                    val_rest0.wait(dve, b, 1 if tiles.stop == HALF else 2)
                val_p1.wait(dve, b, 1 if tiles.stop == HALF else h + 2)
                dve.tensor_tensor(val[:, h % 2, 2, :, tiles], val32[:, :, tiles], val[:, h % 2, 1, :, tiles],
                                  ALU.subtract).then_inc(val_p2.sem, 1)

            def weigh_sums(b, h):
                if h >= 1:
                    head_ok.wait(dve, b, h)
                for k in range(GROUPS):
                    q0, q1 = k * QPB, min(T, (k + 1) * QPB)
                    sums_ps.wait(dve, b, h * GROUPS + k + 1)
                    dve.tensor_tensor(
                        weighted[:, q0:q1], bank[3 * (h % 2) + k][:, 0:(q1 - q0) * 2 * U1].rearrange(
                            "p (q k u) -> p q k u", k=2, u=U1),
                        qry_w[:, :, q0:q1, h:h + 1].rearrange("p k q o -> p q k o").to_broadcast(
                            [P, q1 - q0, 2, U1]), ALU.mult).then_inc(weighted_ok.sem, 1)

            dve.wait_ge(w_in[2], 16)
            with dve.Fori(0, B) as b:
                steps = [0]

                def link(ins):
                    ins.then_inc(chain.sem, 1)
                    steps[0] += 1

                def linked():
                    chain.wait(dve, b, steps[0])

                link(dve.memset(feat[:, :, :, U:U1], 1.0))
                def x_low(t):
                    xt_hi.wait(dve, b, t + 1)
                    c = t % HALF
                    dve.tensor_tensor(trl[:, :, col(c)], bank[t % 2][:].rearrange("p (k n) -> p k n", k=KC),
                                      trh[:, :, col(c)].bitcast(F32), ALU.subtract).then_inc(xt_lo.sem, 1)

                def adj_rows(t):
                    at_ps.wait(dve, b, t + 1)
                    dve.tensor_copy(adj_t[:, :, col(t)],
                                    bank[2 + t % 2][:].bitcast(BF16).rearrange("p (k n) -> p k n", k=T)).then_inc(
                        at_sb.sem, 1)

                def score_low(i):
                    half = slice(i * HALF * P, (i + 1) * HALF * P)
                    sc_hi.wait(dve, b, i + 1)
                    dve.tensor_tensor(sc_hl[32:32 + SC, half], bank[6][0:SC, :],
                                      sc_hl[0:SC, half].bitcast(F32), ALU.subtract).then_inc(sc_lo.sem, 1)

                def feature_rows(t):
                    ft_ps.wait(dve, b, t + 1)
                    dve.tensor_tensor(feat[:, t, :, 0:U], bank[4 + t % 2][:].rearrange("p (h u) -> p h u", h=H),
                                      bias_bc[:].rearrange("p (h u) -> p h u", h=H), ALU.add).then_inc(ft_sb.sem, 1)

                adj_rows(0)
                x_low(0)
                adj_rows(1)
                x_low(1)
                x_low(2)
                adj_rows(2)
                feature_rows(0)
                x_low(3)
                adj_rows(3)
                feature_rows(1)
                adj_rows(4)
                feature_rows(2)
                x_low(4)
                x_low(5)
                score_low(0)
                feature_rows(3)
                x_low(6)
                x_low(7)
                feature_rows(4)
                sc_f32.wait(dve, b, 2)
                link(dve.tensor_reduce(nmax16[:], sc_row[:], AX.X, ALU.max))
                score_low(1)
                linked()
                dve.tensor_scalar(diag16[:], ident[0:SC, 0:SC], nmax16[:, 0:1], None,
                                  ALU.mult).then_inc(diag_ok.sem, 1)
                nat_ps.wait(dve, b, 1)
                dve.tensor_copy(sc_nat[:], bank[7][:, 0:T * SC].rearrange("p (t s) -> p t s", t=T)).then_inc(
                    nat_sb.sem, 1)
                feature_rows(5)
                adj_rows(5)
                adj_rows(6)
                nat_sb.wait(dve, b, 1)
                max_ps.wait(dve, b, 1)
                link(dve.tensor_copy(nmax[:], bank[6][:, 0:SC]))
                linked()
                n_of = nmax[:, H:SC].unsqueeze(1).broadcast_to([P, T, H])
                dve.tensor_tensor(dn[:], sc_nat[:, :, H:SC], n_of, ALU.subtract).then_inc(weights_in.sem, 1)
                link(dve.tensor_tensor(ts[:], sc_nat[:, :, 0:H], n_of, ALU.add))
                dve.tensor_scalar(n_step[:], sc_nat[:, :, H:SC], STEP, None, ALU.mult).then_inc(weights_in.sem, 1)
                linked()
                dve.tensor_scalar(ts_lo[:], ts[:], 0.0, None, ALU.min).then_inc(weights_in.sem, 1)
                dve.tensor_scalar(ts_hi[:], ts[:], 0.0, None, ALU.max).then_inc(weights_in.sem, 1)
                adj_rows(7)
                for s in range(2):
                    dve.wait_ge(y_stored[s], b * (16 * T // 2) + 16)
                at_sb.wait(dve, b, T)
                ft_sb.wait(dve, b, HALF)
                weights.wait(dve, b, 2)
                value_f32(b, 0, FIRST)
                feature_rows(6)
                value_rest0(b, FIRST)

                def mask_upper(g):
                    h, jt = divmod(g, T)
                    stepped.wait(dve, b, g + 1)
                    if g >= MASK_SLOTS:
                        h0, j0 = divmod(g - MASK_SLOTS, T)
                        if j0 == T - 1:
                            sums_ps.wait(dve, b, (h0 + 1) * GROUPS)
                        else:
                            mask_used.wait(dve, b, h0 * (T - 1) + j0 + 1)
                    dve.tensor_tensor(mask[:, 0, g % MASK_SLOTS], step[:, g % STEP_SLOTS], adj_t[:, jt, :],
                                      ALU.min).then_inc(mask1.sem, 1)

                def mask_lower(g):
                    h, jt = divmod(g, T)
                    if not lower_by[h, jt][0]:
                        mask1.wait(dve, b, g + 1)
                        dve.tensor_tensor(mask[:, 1, g % MASK_SLOTS], adj_t[:, jt, :], mask[:, 0, g % MASK_SLOTS],
                                          ALU.subtract).then_inc(mask2_dve.sem, 1)

                mask_upper(0)
                value_p2(b, 0, FIRST)
                mask_lower(0)
                feature_rows(7)
                mask_upper(1)
                ft_sb.wait(dve, b, T)
                value_f32(b, 0, SECOND)
                mask_upper(2)
                value_rest0(b, SECOND)
                mask_lower(2)
                value_p2(b, 0, SECOND)
                for g in range(3, H * T):
                    h, jt = divmod(g, T)
                    mask_upper(g)
                    if g >= 4:
                        mask_lower(g - 1)
                    if jt == (0 if h else 3) and h + 1 < H:
                        value_f32(b, h + 1, FIRST)
                        value_f32(b, h + 1, SECOND)
                    if jt == 2 and h >= 1:
                        weigh_sums(b, h - 1)
                    if jt == 6 and h + 1 < H:
                        value_p2(b, h + 1)
                mask_lower(H * T - 1)
                head_ok.wait(dve, b, H - 1)
                link(dve.reciprocal(rden[:, :, 0:H - 1].unsqueeze(3), feat[:, :, 0:H - 1, U:U1]))
                weigh_sums(b, H - 1)
                weighted_ok.wait(dve, b, H * GROUPS)
                dve.tensor_tensor(feat[:, :, H - 1, :], weighted[:, :, 0, :], weighted[:, :, 1, :],
                                  ALU.add).then_inc(last_head_ok.sem, 1)
                last_head_ok.wait(dve, b, 1)
                dve.reciprocal(rden[:, :, H - 1:H].unsqueeze(3), feat[:, :, H - 1:H, U:U1]).then_inc(rden_ok.sem, 1)
                linked()
                rden_ok.wait(dve, b, 1)
                dve.tensor_tensor(z[:, 0].rearrange("p (h u) -> p h u", h=H), feat[:, 0, :, 0:U],
                                  rden[:, 0, :].unsqueeze(2).broadcast_to([P, H, U]),
                                  ALU.mult).then_inc(ln0_norm.sem, 1)

                def ln0_stats(t):
                    ln0_norm.wait(dve, b, t + 1)
                    dve.scalar_tensor_tensor(out=xs[:, t, :], in0=z[:, t % 2], scalar=0.0, in1=xs[:, t, :],
                                             op0=ALU.max, op1=ALU.add).then_inc(ln0_sum.sem, 1)
                    ln0_sum.wait(dve, b, t + 1)
                    link(dve.bn_stats(stats[:, t % 2], xs[:, t, :]))
                    linked()
                    stand(dve)
                    dve.bn_aggr(mv[:, t, :], stats[:, t % 2]).then_inc(ln0_mv.sem, 1)

                def ln0_factors(t):
                    ln0_sd.wait(dve, b, t + 1)
                    link(dve.reciprocal(rs[:, t:t + 1], sd[:, t:t + 1]))
                    linked()
                    dve.scalar_tensor_tensor(out=nb[:, t:t + 1], in0=mv[:, t, 0:1], scalar=-1.0, in1=rs[:, t:t + 1],
                                             op0=ALU.mult, op1=ALU.mult).then_inc(ln0_nb.sem, 1)

                def x1t_low(t):
                    x1t_hi.wait(dve, b, t + 1)
                    dve.tensor_tensor(x1t_l[:], bank[5][:].rearrange("p (k n) -> p k n", k=KC),
                                      x1t_h[:].bitcast(F32), ALU.subtract).then_inc(x1t_lo.sem, 1)

                for t in range(T):
                    ln0_stats(t)
                    ln0_factors(t)
                    if t == 0:
                        deg_ps.wait(dve, b, 1)
                        dve.tensor_scalar(degc[:], bank[7][:, 0:T], DEG_EPS, None, ALU.max).then_inc(deg_max.sem, 1)
                        deg_max.wait(dve, b, 1)
                        dve.reciprocal(rdeg[:], degc[:]).then_inc(rdeg_ok.sem, 1)
                    if t == 4:
                        x1t_low(0)

                def ln1(t):
                    s = t % 2
                    if t >= 2:
                        y_ok.wait(dve, b, t - 1)
                    o2_sb.wait(dve, b, t + 1)
                    dve.tensor_tensor(z[:, s], bank[O1_BANKS[s]][:], o2s[:, s], ALU.add).then_inc(o_sum.sem, 1)
                    o_sum.wait(dve, b, t + 1)
                    dve.scalar_tensor_tensor(out=z[:, s], in0=z[:, s], scalar=0.0, in1=xs[:, t, :],
                                             op0=ALU.max, op1=ALU.add).then_inc(res_ok.sem, 1)
                    res_ok.wait(dve, b, t + 1)
                    link(dve.bn_stats(stats[:, s], z[:, s]))
                    linked()
                    stand(dve)
                    dve.bn_aggr(mv1[:, s], stats[:, s]).then_inc(ln1_mv.sem, 1)

                def ln1_end(t):
                    s = t % 2
                    ln1_sd.wait(dve, b, t + 1)
                    link(dve.reciprocal(rs1[:, s:s + 1], sd1[:, s:s + 1]))
                    linked()
                    dve.wait_ge(y_stored[s], b * (16 * T // 2) + 16 * (t // 2) + 16)
                    dve.tensor_scalar(y_out[:, s], z[:, s], mv1[:, s, 0:1], rs1[:, s:s + 1],
                                      ALU.subtract, ALU.mult).then_inc(y_ok.sem, 1)

                def agg_low(half):
                    for f in range(KC):
                        aggt_hi.wait(dve, b, half * KC + f + 1)
                        dve.tensor_tensor(trl[:, f, :], bank[AGG_BANKS[half][f]][:], trh[:, f, :].bitcast(F32),
                                          ALU.subtract).then_inc(aggt_lo.sem, 1)

                agg_low(0)
                x1t_low(1)
                for t in range(T):
                    if t == HALF - 1:
                        agg_low(1)
                    ln1(t)
                    if t + 2 < T:
                        x1t_low(t + 2)
                    if t >= 1:
                        ln1_end(t - 1)
                ln1_end(T - 1)
                assert steps[0] == chain.per_batch, steps

        @block.tensor
        def _(pe):
            def mm(o, l, r, start, stop):
                return pe.matmul(o, l, r, start=start, stop=stop, skip_group_check=True)

            pe.wait_ge(consts, 1)
            pe.wait_ge(w_in[3], 16)
            for f in range(2 * KC):
                if f >= 2:
                    pe.wait_ge(w1_lo, f - 1)
                for c in range(KC):
                    ins = pe.transpose(bank[f % 2][:, col(c)], sage_raw[:, c, f * P:(f + 1) * P], ident[:])
                ins.then_inc(w1_ps, 1)
            pe.wait_ge(w1_lo, 2 * KC)
            pe.wait_ge(w_ready, 4)
            pe.wait_ge(consts, N_CONST)

            def split_product(o, lh, ll, rh, rl, first=True, last=True):
                n = len(lh)
                for k in range(n):
                    for i, (a, c) in enumerate(((lh[k], rh[k]), (lh[k], rl[k]), (ll[k], rh[k]))):
                        ins = mm(o, a, c, first and k == 0 and i == 0, last and k == n - 1 and i == 2)
                return ins

            with pe.Fori(0, B) as b:
                def features(t):
                    xt_lo.wait(pe, b, t + 1)
                    if t >= 2:
                        ft_sb.wait(pe, b, t - 1)
                    c = t % HALF
                    split_product(bank[4 + t % 2][:], [trh[:, k, col(c)] for k in range(KC)],
                                  [trl[:, k, col(c)] for k in range(KC)], [w0h[:, k, :] for k in range(KC)],
                                  [w0l[:, k, :] for k in range(KC)]).then_inc(ft_ps.sem, 1)

                def scores(i):
                    xt_lo.wait(pe, b, (i + 1) * HALF)
                    if i == 1:
                        sc_f32.wait(pe, b, 1)
                        sc_lo.wait(pe, b, 1)
                    split_product(bank[6][:], [wah_wide[:, k * SC:k * SC + P] for k in range(KC)],
                                  [wal_wide[:, k * SC:k * SC + P] for k in range(KC)],
                                  [trh[:, k, :] for k in range(KC)],
                                  [trl[:, k, :] for k in range(KC)]).then_inc(sc_ps.sem, 1)

                def turn_x(t):
                    x_in[t].wait(pe, b, 16)
                    if t >= 2:
                        xt_lo.wait(pe, b, t - 1)
                    for k in range(KC):
                        ins = pe.transpose(bank[t % 2][:, col(k)], xs[:, t, col(k)], ident[:])
                    ins.then_inc(xt_ps.sem, 1)

                def turn_adj(t):
                    adj_cast.wait(pe, b, t + 1)
                    if t >= 2:
                        at_sb.wait(pe, b, t - 1)
                    for jt in range(T):
                        ins = pe.transpose(bank[2 + t % 2][:].bitcast(BF16)[:, col(jt)], adj_bf[:, t % 2, col(jt)],
                                           ident_bf[:])
                    ins.then_inc(at_ps.sem, 1)

                turn_adj(0)
                turn_x(0)
                turn_adj(1)
                turn_x(1)
                turn_x(2)
                turn_adj(2)
                features(0)
                turn_x(3)
                turn_adj(3)
                features(1)
                turn_x(4)
                turn_adj(4)
                features(2)
                turn_x(5)
                scores(0)
                features(3)
                turn_x(6)
                turn_x(7)
                features(4)
                scores(1)
                features(5)
                sc_f32.wait(pe, b, 2)
                stand(pe)
                for t in range(T):
                    ins = pe.transpose(bank[7][:, t * SC:(t + 1) * SC], sc_row[:, col(t)], ident[0:SC, 0:SC])
                ins.then_inc(nat_ps.sem, 1)
                turn_adj(5)
                turn_adj(6)
                diag_ok.wait(pe, b, 1)
                sc_lo.wait(pe, b, 2)
                mm(bank[6][:, 0:SC], ones16[:], diag16[:], True, True).then_inc(max_ps.sem, 1)
                turn_adj(7)
                features(6)

                def broadcast(h):
                    if h == 0:
                        nat_sb.wait(pe, b, 1)
                        weights_in.wait(pe, b, 4)
                    else:
                        sb_sb.wait(pe, b, h)
                    for i in range(2):
                        ins = mm(bank[6 + i], pick[:, h:h + 1].to_broadcast([48, P]),
                                 sc_hl[:, i * BANK:(i + 1) * BANK], True, True)
                    ins.then_inc(sb_ps.sem, 1)

                broadcast(0)
                features(7)
                for h in range(H):
                    val_p2.wait(pe, b, h + 2 if h else 1)
                    if h >= 2:
                        weighted_ok.wait(pe, b, (h - 1) * GROUPS)
                    for jt in range(T):
                        g = h * T + jt
                        if h == 0 and jt == HALF:
                            val_p2.wait(pe, b, 2)
                        by_pool, count = lower_by[h, jt]
                        (mask2_pool if by_pool else mask2_dve).wait(pe, b, count)
                        mask1.wait(pe, b, g + 1)
                        for q in range(T):
                            k, i = divmod(q, QPB)
                            for kind in range(2):
                                at = (2 * i + kind) * U1
                                for part in range(PARTS):
                                    ins = mm(bank[3 * (h % 2) + k][:, at:at + U1],
                                             mask[:, kind, g % MASK_SLOTS, col(q)],
                                             val[:, h % 2, part, kind, jt, :],
                                             jt == 0 and i == 0 and kind == 0 and part == 0,
                                             jt == T - 1)
                            if jt == T - 1 and (i == QPB - 1 or q == T - 1):
                                ins.then_inc(sums_ps.sem, 1)
                        if jt < T - 1:
                            ins.then_inc(mask_used.sem, 1)
                        if jt == 1 and h + 1 < H:
                            broadcast(h + 1)
                    if h == H - 1:
                        sb_sb.wait(pe, b, H)
                        for q in range(T):
                            for jt in range(T):
                                ins = mm(bank[7][:, q:q + 1], adj_t[:, jt, col(q)], ones_bf[:], jt == 0, jt == T - 1)
                        ins.then_inc(deg_ps.sem, 1)

                def aggregate(half, f, jt):
                    for i, r in enumerate((x1h, x1l)):
                        ins = mm(bank[AGG_BANKS[half][f]][:], r[:, jt, col(f)],
                                 adj_t[:, jt, half * HALF * P:(half + 1) * HALF * P],
                                 jt == 0 and i == 0, jt == T - 1 and i == 1)
                    if jt == T - 1:
                        ins.then_inc(agg_ps.sem, 1)

                def turn_x1(t):
                    if t >= 1:
                        x1t_lo.wait(pe, b, t)
                    for k in range(KC):
                        ins = pe.transpose(bank[5][:, col(k)], xs[:, t, col(k)], ident[:])
                    ins.then_inc(x1t_ps.sem, 1)

                def own(t):
                    x1t_lo.wait(pe, b, t + 1)
                    if t >= 2:
                        o_sum.wait(pe, b, t - 1)
                    split_product(bank[O1_BANKS[t % 2]][:], [x1t_h[:, k, :] for k in range(KC)],
                                  [x1t_l[:, k, :] for k in range(KC)], [w1h[:, k, :] for k in range(KC)],
                                  [w1l[:, k, :] for k in range(KC)]).then_inc(o1_ps.sem, 1)

                def neighbours(t):
                    aggt_lo.wait(pe, b, (t // HALF + 1) * KC)
                    if t >= 1:
                        o2_sb.wait(pe, b, t)
                    c = t % HALF
                    split_product(bank[2][:], [trh[:, k, col(c)] for k in range(KC)],
                                  [trl[:, k, col(c)] for k in range(KC)], [w1h[:, KC + k, :] for k in range(KC)],
                                  [w1l[:, KC + k, :] for k in range(KC)]).then_inc(o2_ps.sem, 1)

                for jt in range(T):
                    x1_lo.wait(pe, b, jt + 1)
                    for f in range(KC):
                        aggregate(0, f, jt)
                    if jt == 0:
                        deg_max.wait(pe, b, 1)
                    for f in range(2):
                        aggregate(1, f, jt)
                    if jt == 1:
                        turn_x1(0)
                    if jt == 4:
                        own(0)
                turn_x1(1)
                for t in range(T):
                    if t < 2:
                        aggt_lo.wait(pe, b, t + 1)
                        for jt in range(T):
                            aggregate(1, 2 + t, jt)
                    neighbours(t)
                    if t + 1 < T:
                        own(t + 1)
                    if t + 2 < T:
                        turn_x1(t + 2)
                res_ok.wait(pe, b, T)


_INS = ["x", "adj", "L0_gnn_W", "L0_gnn_b", "L0_gnn_a_self", "L0_gnn_a_neigh", "L1_gnn_W"]


def kernel(**inputs):
    import numpy as _np
    import concourse.bacc as _bacc
    from concourse import mybir as _mybir
    from concourse.bass_utils import run_bass_kernel_spmd as _run

    nc = _bacc.Bacc("TRN2", target_bir_lowering=False, num_devices=1)
    arrays, args = {}, []
    for name in _INS:
        a = _np.ascontiguousarray(inputs[name])
        arrays[f"in_{name}_dram"] = a
        args.append(nc.dram_tensor(f"in_{name}_dram", a.shape, _mybir.dt.from_np(a.dtype), kind="ExternalInput").ap())
    out = nc.dram_tensor("out_0_dram", inputs["x"].shape, _mybir.dt.float32, kind="ExternalOutput").ap()
    gat_sage_kernel(nc, *args, out)
    r = _run(nc, [arrays], core_ids=[0])
    return r.results[0]["out_0_dram"]
```

```python
from contextlib import ExitStack

import concourse.bass as bass
from concourse import mybir

F32 = mybir.dt.float32
F32R = mybir.dt.float32r
BF16 = mybir.dt.bfloat16
F16 = mybir.dt.float16
ALU = mybir.AluOpType
ACT = mybir.ActivationFunctionType
AX = mybir.AxisListType

P = 128
LN_EPS = 1e-5
DEG_EPS = 1e-6
SLOPE = 0.2
STEP = 2.0 ** 100
X1_SCALE = 2.0 ** 11
MASK_SLOTS = 6
STEP_SLOTS = 3
PARTS = 3


class Signal:

    def __init__(self, sem, per_batch):
        self.sem, self.per_batch = sem, per_batch

    def at(self, batch, count):
        assert 0 < count <= self.per_batch
        return batch * self.per_batch + count


def gat_sage_kernel(nc, x, adj, gat_w, gat_b, gat_self, gat_neigh, sage_w, out):
    B, N, D = x.shape
    H, _, U = gat_w.shape
    T = N // P
    KC = D // P
    HALF = T // 2
    U1 = U + 1
    HU = H * U
    SC = 2 * H
    BANK = 512
    TPB = BANK // P
    QPB = 3
    GROUPS = (T + QPB - 1) // QPB
    lower_by, made = {}, [0, 0]
    for h in range(H):
        for jt in range(T):
            by_pool = jt in ((0,) if h == 0 else (1, 4) if h == H - 1 else (5,))
            made[by_pool] += 1
            lower_by[h, jt] = by_pool, made[by_pool]
    NDVE, NPOOL = made
    AGG_BANKS = ((0, 1, 2, 6), (7, 3, 0, 1))
    O1_BANKS = (4, 6)
    EARLY = 4
    ADJ_BANKS = (3, 2)
    FIRST, SECOND = slice(0, HALF), slice(HALF, T)
    CHAIN = 4 + 4 * T

    with ExitStack() as ctx:
        def sb(name, shape, dt):
            return ctx.enter_context(nc.sbuf_tensor(name, shape, dt))

        def sem(name):
            return ctx.enter_context(nc.semaphore(name))

        ident = sb("ident", [P, P], F32)
        ident_bf = sb("ident_bf", [P, P], BF16)
        ones_bf = sb("ones_bf", [P, 1], BF16)
        ones16 = sb("ones16", [SC, P], F32)
        bias_bc = sb("bias_bc", [P, HU], F32)
        w0h = sb("w0h", [P, KC, HU], F32R)
        w0l = sb("w0l", [P, KC, HU], F32R)
        wah_wide = sb("wah_wide", [P, (KC - 1) * SC + P], F32R)
        wal_wide = sb("wal_wide", [P, (KC - 1) * SC + P], F32R)
        wah, wal = (w[:, 0:KC * SC].rearrange("p (c n) -> p c n", c=KC) for w in (wah_wide, wal_wide))
        w1h = sb("w1h", [P, 2 * KC, D], F32R)
        w1l = sb("w1l", [P, 2 * KC, D], F32R)
        xs = sb("xs", [P, T, D], F32)
        x1_parts = sb("x1_parts", [P, 2, T, D], F16)
        x1h, x1l = x1_parts[:, 0], x1_parts[:, 1]
        heads32 = x1_parts[:, :, :, :].rearrange("p k t d -> p (k t d)").bitcast(F32)

        HEAD = 2 * T * U1
        val32 = [heads32[:, i * HEAD:(i + 1) * HEAD].rearrange("p (k t u) -> p k t u", k=2, t=T) for i in range(2)]
        weighted = heads32[:, T * D - HEAD:T * D].rearrange("p (t k u) -> p t k u", k=2, u=U1)
        feat = sb("feat", [P, T, H, U1], F32)
        trh = sb("trh", [P, KC, HALF * P], F32R)
        trl = sb("trl", [P, KC, HALF * P], F32R)
        adj_nat = sb("adj_nat", [P, 2, N], F32)
        adj_bf = sb("adj_bf", [P, 2, N], BF16)
        adj_t = sb("adj_t", [P, T, N], BF16)
        sc_row = sb("sc_row", [SC, N], F32)
        s_bc = sb("s_bc", [P, 2, N], F32)
        x1t_h = sb("x1t_h", [P, KC, P], F32R)
        x1t_l = sb("x1t_l", [P, KC, P], F32R)
        step = sb("step", [P, STEP_SLOTS, N], BF16)
        mask = sb("mask", [P, 2, MASK_SLOTS, N], BF16)
        val = sb("val", [P, 2, PARTS, 2, T, U1], BF16)
        sc_nat = sb("sc_nat", [P, T, SC], F32)
        nmax16 = sb("nmax16", [SC, 1], F32)
        diag16 = sb("diag16", [SC, SC], F32)
        nmax = sb("nmax", [P, SC], F32)
        n_step = sb("n_step", [P, T, H], F32)
        dn = sb("dn", [P, T, H], F32)
        ts = sb("ts", [P, T, H], F32)
        ts_lo = sb("ts_lo", [P, T, H], F32)
        ts_hi = sb("ts_hi", [P, T, H], F32)
        key_w = sb("key_w", [P, 2, T, H], F32)
        qry_w = sb("qry_w", [P, 2, T, H], F32)
        rden = sb("rden", [P, T, H], F32)
        z = s_bc[:, 0].rearrange("p (s d) -> p s d", s=2)
        stats = sb("stats", [P, 2, 6], F32)
        mv = sb("mv", [P, T, 2], F32)
        sd = sb("sd", [P, T], F32)
        rs = sb("rs", [P, T], F32)
        mv1 = sb("mv1", [P, 2, 2], F32)
        sd1 = sb("sd1", [P, 2], F32)
        rs1 = sb("rs1", [P, 2], F32)
        degc = sb("degc", [P, T], F32)
        eps = sb("eps", [P, 2], F32)
        nb = sb("nb", [P, T], F32)
        rdeg = sb("rdeg", [P, T], F32)
        mask32 = mask[:, :, :, :].rearrange("p k s n -> p (k s n)").bitcast(F32)
        o2s = mask32[:, 0:2 * D].rearrange("p (s d) -> p s d", s=2)
        y_out = mask32[:, 2 * D:4 * D].rearrange("p (s d) -> p s d", s=2)
        w_raw = feat[:, 0:4, :, :].rearrange("p a b c -> p (a b c)")[:, 0:KC * HU].rearrange(
            "p (c n) -> p c n", c=KC)
        a_bc = z
        prod = y_out
        wa32 = sb("wa32", [P, KC, SC], F32)
        sage_raw = xs[:, :, :].rearrange("p t d -> p (t d)").rearrange("p (c f) -> p c f", c=KC)

        bank = [ctx.enter_context(nc.psum_tensor(f"bank{k}", [P, BANK], F32)) for k in range(8)]

        w_in = [sem(f"w_in{k}") for k in range(4)]
        pool_const, consts = sem("pool_const"), sem("consts")
        w_ready, w1_ps, w1_hi, w1_lo, wa_step = (
            sem("w_ready"), sem("w1_ps"), sem("w1_hi"), sem("w1_lo"), sem("wa_step"))
        x_in = [Signal(sem(f"x_in{t}"), 16) for t in range(T)]
        a_in = [sem(f"a_in{s}") for s in range(2)]
        y_stored = [sem(f"y_stored{s}") for s in range(2)]

        def signal(name, per_batch):
            return Signal(sem(name), per_batch)

        xt_ps = signal("xt_ps", T)
        xt_hi = signal("xt_hi", T)
        xt_lo = signal("xt_lo", T)
        adj_cast = signal("adj_cast", T)
        at_ps = signal("at_ps", T)
        at_sb = signal("at_sb", T)
        ft_ps = signal("ft_ps", T)
        ft_sb = signal("ft_sb", T)
        sc_ps = signal("sc_ps", 2)
        sc_f32 = signal("sc_f32", 2)
        nat_ps = signal("nat_ps", 1)
        nat_sb = signal("nat_sb", 1)
        diag_ok = signal("diag_ok", 1)
        max_ps = signal("max_ps", 1)
        weights_in = signal("weights_in", 4)
        weights = signal("weights", 4)
        ones_ok = signal("ones_ok", 1)
        chain = signal("chain", CHAIN)
        s_stored = signal("s_stored", 2 * 16)
        s_in = [signal(f"s_in{i}", 16 * H // 2) for i in range(2)]
        stepped = signal("stepped", H * T)
        mask1 = signal("mask1", H * T)
        mask2_dve = signal("mask2_dve", NDVE)
        mask2_pool = signal("mask2_pool", NPOOL)
        mask_used = signal("mask_used", H * (T - 1))
        val_f32_0 = signal("val_f32_0", 1)
        val_f32 = signal("val_f32", H)
        val_p0 = signal("val_p0", H + 1)
        val_rest0 = signal("val_rest0", 2)
        val_rest = signal("val_rest", H - 1)
        val_p1 = signal("val_p1", H + 1)
        val_p2 = signal("val_p2", 3)
        val_p2_pool = signal("val_p2_pool", H - 2)
        sums_ps = signal("sums_ps", H * GROUPS)
        weighted_ok = signal("weighted_ok", H * GROUPS)
        head_ok = signal("head_ok", H - 1)
        last_head_ok = signal("last_head_ok", 2)
        deg_ps = signal("deg_ps", 1)
        deg_max = signal("deg_max", 1)
        rdeg_ok = signal("rdeg_ok", 1)
        rden_ok = signal("rden_ok", 2)
        ln0_norm = signal("ln0_norm", T)
        ln0_sum = signal("ln0_sum", T)
        ln0_mv = signal("ln0_mv", T)
        ln0_sd = signal("ln0_sd", T)
        ln0_nb = signal("ln0_nb", T)
        x1_ok = signal("x1_ok", T)
        x1_hi = signal("x1_hi", T)
        x1_lo = signal("x1_lo", T)
        agg_ps = signal("agg_ps", 2 * KC)
        aggt_hi = signal("aggt_hi", 2 * KC)
        aggt_lo = signal("aggt_lo", 2 * KC)
        x1t_ps = signal("x1t_ps", T)
        x1t_hi = signal("x1t_hi", T)
        x1t_lo = signal("x1t_lo", T)
        o1_ps = signal("o1_ps", T)
        o2_ps = signal("o2_ps", T)
        o2_sb = signal("o2_sb", T)
        o_sum = signal("o_sum", T)
        res_ok = signal("res_ok", T)
        ln1_mv = signal("ln1_mv", T)
        ln1_sd = signal("ln1_sd", T)
        y_ok = signal("y_ok", T)

        def rows(v):
            return v.rearrange("h u -> (h u)").partition_broadcast(P)

        s_dram = nc.dram_tensor("self_scores", [H, N], F32, kind="Internal").ap()

        def col(c):
            return slice(c * P, (c + 1) * P)

        N_CONST = 8
        turnstile = sem("turnstile")

        def stand(engine):
            engine.sem_inc(turnstile, 1)

        block = ctx.enter_context(nc.Block())

        @block.sync
        def _(sp):
            for c in range(KC):
                sp.dma_start(w_raw[:, c, :].rearrange("p (h u) -> p h u", h=H),
                             gat_w[:, col(c), :].rearrange("h p u -> p h u")).then_inc(w_in[0], 16)
            sp.dma_start(a_bc[:, 0, :], rows(gat_self)).then_inc(w_in[1], 16)
            sp.dma_start(a_bc[:, 1, :], rows(gat_neigh)).then_inc(w_in[1], 16)
            sp.dma_start(bias_bc[:, :], rows(gat_b)).then_inc(w_in[2], 16)
            sp.dma_start(sage_raw, sage_w.rearrange("(c p) f -> p c f", p=P)).then_inc(w_in[3], 16)
            sp.sem_inc(y_stored[0], 16)
            sp.sem_inc(y_stored[1], 16)

            def load_x(b, t):
                sp.dma_start(xs[:, t, :], x[b, t * P:(t + 1) * P, :]).then_inc(x_in[t].sem, 16)

            def load_adj(b, t):
                sp.dma_start(adj_nat[:, t % 2, :], adj[b, t * P:(t + 1) * P, :]).then_inc(a_in[t % 2], 16)

            def store_y(b, t):
                sp.wait_ge(y_ok.sem, y_ok.at(b, t + 1))
                sp.dma_start(out[b, t * P:(t + 1) * P, :], y_out[:, t % 2, :]).then_inc(y_stored[t % 2], 16)

            def load_late_adj(b, tiles):
                for t in tiles:
                    sp.wait_ge(adj_cast.sem, adj_cast.at(b, t - 1))
                    load_adj(b, t)

            def store_scores(b, i):
                sp.wait_ge(sc_f32.sem, sc_f32.at(b, i + 1))
                half = slice(i * HALF * P, (i + 1) * HALF * P)
                sp.dma_start(s_dram[:, half], sc_row[0:H, half]).then_inc(s_stored.sem, 16)

            def load_scores(b, h):
                if h >= 2:
                    sp.wait_ge(stepped.sem, stepped.at(b, (h - 1) * T))
                sp.dma_start(s_bc[:, h % 2], s_dram[h].partition_broadcast(P)).then_inc(s_in[h % 2].sem, 16)

            def first_scores(b):
                store_scores(b, 1)
                sp.wait_ge(s_stored.sem, s_stored.at(b, 32))
                load_scores(b, 0)
                load_scores(b, 1)

            for t in range(2):
                load_adj(0, t)
            sp.wait_ge(w1_ps, 2 * KC)
            for t in range(T):
                load_x(0, t)
            load_late_adj(0, range(2, 7))
            store_scores(0, 0)
            load_late_adj(0, (7,))
            with sp.Fori(0, B - 1) as b:
                first_scores(b)
                for t in range(2):
                    sp.wait_ge(adj_cast.sem, adj_cast.at(b, T - 1 + t))
                    load_adj(b + 1, t)
                for h in range(2, H):
                    load_scores(b, h)
                for t in range(T):
                    if t == T - 1:
                        load_late_adj(b + 1, (2, 3))
                    sp.wait_ge(res_ok.sem, res_ok.at(b, t + 1))
                    load_x(b + 1, t)
                    if t >= 2:
                        store_y(b, t - 2)
                load_late_adj(b + 1, (4,))
                store_y(b, T - 2)
                store_y(b, T - 1)
                load_late_adj(b + 1, (5, 6))
                store_scores(b + 1, 0)
                load_late_adj(b + 1, (7,))
            first_scores(B - 1)
            for h in range(2, H):
                load_scores(B - 1, h)
            for t in range(T):
                store_y(B - 1, t)
            for s in range(2):
                sp.wait_ge(y_stored[s], 16 * (B * T // 2 + 1))

        @block.gpsimd
        def _(pool):
            pool.memset(ident[:], 0.0).then_inc(pool_const, 1)
            pool.wait_ge(pool_const, 1)
            pool.affine_select(out=ident[:], in_=ident[:], compare_op=ALU.not_equal, fill=1.0, base=0,
                               pattern=[[-1, P]], channel_multiplier=1).then_inc(consts, 1)
            pool.wait_ge(consts, 1)
            pool.tensor_copy(ident_bf[:], ident[:]).then_inc(consts, 1)
            pool.memset(ones16[:], 1.0).then_inc(consts, 1)
            pool.memset(ones_bf[:], 1.0).then_inc(consts, 1)
            pool.memset(eps[:, 0:1], LN_EPS / X1_SCALE ** 2).then_inc(consts, 1)
            pool.memset(eps[:, 1:2], LN_EPS * X1_SCALE ** 2).then_inc(consts, 1)
            pool.memset(wah_wide[:].bitcast(F32), 0.0).then_inc(consts, 1)
            pool.memset(wal_wide[:].bitcast(F32), 0.0).then_inc(consts, 1)

            def value_f32(b, h, tiles=slice(0, T)):
                if 2 <= h < 4:
                    pool.wait_ge(val_p2.sem, val_p2.at(b, h))
                elif h >= 4:
                    pool.wait_ge(val_p2_pool.sem, val_p2_pool.at(b, h - 3))
                n = tiles.stop - tiles.start
                pool.tensor_tensor(val32[h % 2][:, :, tiles],
                                   feat[:, tiles, h, :].unsqueeze(1).broadcast_to([P, 2, n, U1]),
                                   key_w[:, :, tiles, h:h + 1].to_broadcast([P, 2, n, U1]),
                                   ALU.mult).then_inc(val_f32.sem, 1)

            def value_rest(b, h):
                pool.wait_ge(val_f32.sem, val_f32.at(b, h + 1))
                pool.wait_ge(val_p0.sem, val_p0.at(b, h + 2))
                v = val32[h % 2]
                pool.tensor_tensor(v, v, val[:, h % 2, 0], ALU.subtract).then_inc(val_rest.sem, 1)

            def value_p2(b, h):
                pool.wait_ge(val_p1.sem, val_p1.at(b, h + 2))
                pool.tensor_tensor(val[:, h % 2, 2], val32[h % 2], val[:, h % 2, 1],
                                   ALU.subtract).then_inc(val_p2_pool.sem, 1)

            def add_branches(b, h):
                pool.wait_ge(weighted_ok.sem, weighted_ok.at(b, (h + 1) * GROUPS))
                pool.tensor_tensor(feat[:, :, h, :], weighted[:, :, 0, :], weighted[:, :, 1, :],
                                   ALU.add).then_inc(head_ok.sem, 1)

            with pool.Fori(0, B) as b:
                def mask_lower(h, jt):
                    g = h * T + jt
                    pool.wait_ge(mask1.sem, mask1.at(b, g + 1))
                    pool.tensor_tensor(mask[:, 1, g % MASK_SLOTS], adj_t[:, jt, :], mask[:, 0, g % MASK_SLOTS],
                                       ALU.subtract).then_inc(mask2_pool.sem, 1)

                for h in range(H):
                    keys = [jt for jt in range(T) if lower_by[h, jt][0]]
                    if h == 0:
                        mask_lower(h, keys[0])
                        pool.wait_ge(ft_sb.sem, ft_sb.at(b, T))
                        pool.wait_ge(weights.sem, weights.at(b, 2))
                        pool.wait_ge(ones_ok.sem, ones_ok.at(b, 1))
                        value_f32(b, 0, SECOND)
                        value_f32(b, 1)
                        value_rest(b, 1)
                    elif h < H - 1:
                        value_f32(b, h + 1)
                        value_rest(b, h + 1)
                        mask_lower(h, keys[0])
                        value_p2(b, h + 1)
                        add_branches(b, h - 1)
                    else:
                        for jt in keys:
                            mask_lower(h, jt)
                        add_branches(b, h - 1)

                def norm(t):
                    if t >= 2:
                        pool.wait_ge(ln0_sum.sem, ln0_sum.at(b, t - 1))
                    pool.tensor_tensor(z[:, t % 2].rearrange("p (h u) -> p h u", h=H), feat[:, t, :, 0:U],
                                       rden[:, t, :].unsqueeze(2).broadcast_to([P, H, U]),
                                       ALU.mult).then_inc(ln0_norm.sem, 1)

                def x1_low(t):
                    pool.wait_ge(x1_ok.sem, x1_ok.at(b, t + 1))
                    pool.tensor_tensor(x1l[:, t, :], xs[:, t, :], x1h[:, t, :], ALU.subtract).then_inc(x1_lo.sem, 1)

                pool.wait_ge(rden_ok.sem, rden_ok.at(b, 1))
                pool.wait_ge(last_head_ok.sem, last_head_ok.at(b, 1))
                pool.wait_ge(ln0_norm.sem, ln0_norm.at(b, 1))
                norm(1)
                norm(2)
                for t in range(T):
                    x1_low(t)
                    if t == 0:
                        pool.wait_ge(rden_ok.sem, rden_ok.at(b, 2))
                        pool.wait_ge(last_head_ok.sem, last_head_ok.at(b, 2))
                    if t + 3 < T:
                        norm(t + 3)

        @block.scalar
        def _(act):
            def copy(o, i, scale=1.0):
                return act.activation(o, i, ACT.Copy, scale=scale)

            for c in range(2 * KC):
                act.wait_ge(w1_ps, c + 1)
                copy(w1h[:, c, :], bank[c % 2][:]).then_inc(w1_hi, 1)

            def value_p0(b, h, tiles=slice(0, T)):
                if tiles.stop == HALF:
                    act.wait_ge(val_f32_0.sem, val_f32_0.at(b, 1))
                else:
                    act.wait_ge(val_f32.sem, val_f32.at(b, h + 1))
                if h >= 2:
                    act.wait_ge(sums_ps.sem, sums_ps.at(b, (h - 1) * GROUPS))
                copy(val[:, h % 2, 0, :, tiles], val32[h % 2][:, :, tiles]).then_inc(val_p0.sem, 1)

            def value_p1(b, h, tiles=slice(0, T)):
                if h == 0:
                    act.wait_ge(val_rest0.sem, val_rest0.at(b, 1 if tiles.stop == HALF else 2))
                else:
                    act.wait_ge(val_rest.sem, val_rest.at(b, h))
                copy(val[:, h % 2, 1, :, tiles], val32[h % 2][:, :, tiles]).then_inc(val_p1.sem, 1)

            def x_high(b, t):
                act.wait_ge(xt_ps.sem, xt_ps.at(b, t + 1))
                if t == HALF:
                    act.wait_ge(sc_ps.sem, sc_ps.at(b, 1))
                if t >= HALF:
                    act.wait_ge(ft_ps.sem, ft_ps.at(b, t - HALF + 1))
                copy(trh[:, :, col(t % HALF)],
                     bank[t % 2][:].rearrange("p (k n) -> p k n", k=KC)).then_inc(xt_hi.sem, 1)

            def cast_adj(b, t):
                act.wait_ge(a_in[t % 2], b * (16 * T // 2) + 16 * (t // 2) + 16)
                if t >= 2:
                    act.wait_ge(at_ps.sem, at_ps.at(b, t - 1))
                copy(adj_bf[:, t % 2], adj_nat[:, t % 2]).then_inc(adj_cast.sem, 1)

            def batch(b, more):
                def score_rows(i):
                    act.wait_ge(sc_ps.sem, sc_ps.at(b, i + 1))
                    half = slice(i * HALF * P, (i + 1) * HALF * P)
                    copy(sc_row[:, half], bank[6][0:SC, :]).then_inc(sc_f32.sem, 1)

                def make_step(g):
                    h, jt = divmod(g, T)
                    if g >= STEP_SLOTS:
                        act.wait_ge(mask1.sem, mask1.at(b, g - STEP_SLOTS + 1))
                    if jt == 0:
                        loaded = s_in[h % 2]
                        act.wait_ge(loaded.sem, loaded.at(b, 16 * (h // 2 + 1)))
                        stand(act)
                    act.activation(step[:, g % STEP_SLOTS], s_bc[:, h % 2], ACT.Relu, scale=STEP,
                                   bias=n_step[:, jt, h:h + 1]).then_inc(stepped.sem, 1)

                def weight_exp(o, a, k):
                    act.wait_ge(weights_in.sem, weights_in.at(b, 4))
                    act.activation(o, a[:], ACT.Exp, scale=k).then_inc(weights.sem, 1)

                x_high(b, 2)
                cast_adj(b, 3)
                x_high(b, 3)
                cast_adj(b, 4)
                x_high(b, 4)
                x_high(b, 5)
                score_rows(0)
                x_high(b, 6)
                x_high(b, 7)
                cast_adj(b, 5)
                cast_adj(b, 6)
                score_rows(1)
                cast_adj(b, 7)
                weight_exp(key_w[:, 0], dn, 1.0)
                weight_exp(key_w[:, 1], dn, SLOPE)
                weight_exp(qry_w[:, 0], ts_lo, 1.0 - SLOPE)
                weight_exp(qry_w[:, 1], ts_hi, SLOPE - 1.0)
                value_p0(b, 0, FIRST)
                make_step(0)
                value_p1(b, 0, FIRST)
                for g in range(1, 5):
                    make_step(g)
                value_p0(b, 0, SECOND)
                make_step(5)
                value_p1(b, 0, SECOND)
                for h in range(H):
                    for jt in range(T):
                        g = h * T + jt
                        if jt == 6 and h == 0:
                            value_p0(b, 1)
                        if g >= 6:
                            make_step(g)
                        if jt == 4 and 1 <= h < H - 1:
                            value_p0(b, h + 1)
                        if jt == (6 if h else 7) and h + 1 < H:
                            value_p1(b, h + 1)

                def x1_parts_of(t):
                    act.wait_ge(ln0_nb.sem, ln0_nb.at(b, t + 1))
                    act.activation(x1h[:, t, :], xs[:, t, :], ACT.Identity, bias=nb[:, t:t + 1],
                                   scale=rs[:, t:t + 1]).then_inc(x1_hi.sem, 1)
                    act.wait_ge(x1_hi.sem, x1_hi.at(b, t + 1))
                    act.activation(xs[:, t, :], xs[:, t, :], ACT.Identity, bias=nb[:, t:t + 1],
                                   scale=rs[:, t:t + 1]).then_inc(x1_ok.sem, 1)

                def x1t_high(t):
                    act.wait_ge(x1t_ps.sem, x1t_ps.at(b, t + 1))
                    if t >= 1:
                        act.wait_ge(o1_ps.sem, o1_ps.at(b, t))
                    copy(x1t_h[:], bank[5][:].rearrange("p (k n) -> p k n", k=KC)).then_inc(x1t_hi.sem, 1)

                for t in range(T):
                    act.wait_ge(ln0_mv.sem, ln0_mv.at(b, t + 1))
                    act.activation(sd[:, t:t + 1], mv[:, t, 1:2], ACT.Sqrt, bias=eps[:, 0:1],
                                   scale=1.0 / X1_SCALE ** 2).then_inc(ln0_sd.sem, 1)
                    x1_parts_of(t)
                    if t == 3:
                        x1t_high(0)

                def agg_high(half):
                    for f in range(KC):
                        act.wait_ge(agg_ps.sem, agg_ps.at(b, half * KC + f + 1))
                        copy(trh[:, f, :], bank[AGG_BANKS[half][f]][:]).then_inc(aggt_hi.sem, 1)

                def by_degree(t):
                    if t == 0:
                        act.wait_ge(rdeg_ok.sem, rdeg_ok.at(b, 1))
                    act.wait_ge(o2_ps.sem, o2_ps.at(b, t + 1))
                    if t >= 2:
                        act.wait_ge(o_sum.sem, o_sum.at(b, t - 1))
                    copy(o2s[:, t % 2], bank[2][:], rdeg[:, t:t + 1]).then_inc(o2_sb.sem, 1)

                def ln1_root(t):
                    act.wait_ge(ln1_mv.sem, ln1_mv.at(b, t + 1))
                    act.activation(sd1[:, t % 2:t % 2 + 1], mv1[:, t % 2, 1:2], ACT.Sqrt,
                                   bias=eps[:, 1:2]).then_inc(ln1_sd.sem, 1)

                agg_high(0)
                x1t_high(1)
                for t in range(T):
                    if more and t == T - 1:
                        cast_adj(b + 1, 0)
                        cast_adj(b + 1, 1)
                    by_degree(t)
                    if t == HALF - 1:
                        agg_high(1)
                    if t + 2 < T:
                        x1t_high(t + 2)
                    if t >= 1:
                        ln1_root(t - 1)
                if more:
                    x_high(b + 1, 0)
                    cast_adj(b + 1, 2)
                    x_high(b + 1, 1)
                ln1_root(T - 1)

            cast_adj(0, 0)
            cast_adj(0, 1)
            x_high(0, 0)
            cast_adj(0, 2)
            x_high(0, 1)
            with act.Fori(0, B - 1) as b:
                batch(b, True)
            batch(B - 1, False)

        @block.vector
        def _(dve):
            dve.wait_ge(w_in[0], 16 * KC)
            dve.tensor_copy(w0h[:], w_raw).then_inc(w_ready, 1)
            dve.wait_ge(w_ready, 1)
            dve.tensor_tensor(w0l[:], w_raw, w0h[:].bitcast(F32), ALU.subtract).then_inc(w_ready, 1)
            dve.wait_ge(w_in[1], 32)
            dve.wait_ge(consts, N_CONST)
            n = 0
            for c in range(KC):
                for k in range(2):
                    dve.tensor_tensor(prod[:, 0], w_raw[:, c, :], a_bc[:, k, :], ALU.mult).then_inc(wa_step, 1)
                    dve.wait_ge(wa_step, n + 1)
                    dve.tensor_reduce(wa32[:, c, k * H:(k + 1) * H], prod[:, 0].rearrange("p (h u) -> p h u", h=H),
                                      AX.X, ALU.add).then_inc(wa_step, 1)
                    dve.wait_ge(wa_step, n + 2)
                    n += 2
            dve.tensor_copy(wah, wa32[:]).then_inc(w_ready, 1)
            dve.wait_ge(w_ready, 3)
            dve.tensor_tensor(wal, wa32[:], wah.bitcast(F32),
                              ALU.subtract).then_inc(w_ready, 1)
            for c in range(2 * KC):
                dve.wait_ge(w1_hi, c + 1)
                dve.tensor_tensor(w1l[:, c, :], bank[c % 2][:], w1h[:, c, :].bitcast(F32),
                                  ALU.subtract).then_inc(w1_lo, 1)

            def value_f32_0(b):
                dve.tensor_tensor(val32[0][:, :, FIRST],
                                  feat[:, FIRST, 0, :].unsqueeze(1).broadcast_to([P, 2, HALF, U1]),
                                  key_w[:, :, FIRST, 0:1].to_broadcast([P, 2, HALF, U1]),
                                  ALU.mult).then_inc(val_f32_0.sem, 1)

            def value_rest0(b, tiles):
                count = 1 if tiles.stop == HALF else 2
                dve.wait_ge(val_p0.sem, val_p0.at(b, count))
                values_ok = val_f32_0 if tiles.stop == HALF else val_f32
                dve.wait_ge(values_ok.sem, values_ok.at(b, 1))
                v = val32[0][:, :, tiles]
                dve.tensor_tensor(v, v, val[:, 0, 0, :, tiles], ALU.subtract).then_inc(val_rest0.sem, 1)

            def value_p2(b, h, tiles=slice(0, T)):
                if h == 0:
                    dve.wait_ge(val_rest0.sem, val_rest0.at(b, 1 if tiles.stop == HALF else 2))
                dve.wait_ge(val_p1.sem, val_p1.at(b, 1 if tiles.stop == HALF else h + 2))
                dve.tensor_tensor(val[:, h % 2, 2, :, tiles], val32[h % 2][:, :, tiles], val[:, h % 2, 1, :, tiles],
                                  ALU.subtract).then_inc(val_p2.sem, 1)

            def weigh_sums(b, h, groups=range(GROUPS)):
                if h >= 1:
                    dve.wait_ge(head_ok.sem, head_ok.at(b, h))
                for k in groups:
                    q0, q1 = k * QPB, min(T, (k + 1) * QPB)
                    dve.wait_ge(sums_ps.sem, sums_ps.at(b, h * GROUPS + k + 1))
                    dve.tensor_tensor(
                        weighted[:, q0:q1], bank[3 * (h % 2) + k][:, 0:(q1 - q0) * 2 * U1].rearrange(
                            "p (q k u) -> p q k u", k=2, u=U1),
                        qry_w[:, :, q0:q1, h:h + 1].rearrange("p k q o -> p q k o").to_broadcast(
                            [P, q1 - q0, 2, U1]), ALU.mult).then_inc(weighted_ok.sem, 1)

            def ones_column(b):
                dve.memset(feat[:, :, :, U:U1], 1.0).then_inc(ones_ok.sem, 1)

            def x_low(b, t):
                dve.wait_ge(xt_hi.sem, xt_hi.at(b, t + 1))
                c = t % HALF
                dve.tensor_tensor(trl[:, :, col(c)], bank[t % 2][:].rearrange("p (k n) -> p k n", k=KC),
                                  trh[:, :, col(c)].bitcast(F32), ALU.subtract).then_inc(xt_lo.sem, 1)

            def adj_rows(b, t):
                dve.wait_ge(at_ps.sem, at_ps.at(b, t + 1))
                dve.tensor_copy(adj_t[:, :, col(t)],
                                bank[ADJ_BANKS[t % 2]][:].bitcast(BF16).rearrange("p (k n) -> p k n", k=T)).then_inc(
                    at_sb.sem, 1)

            def batch(b, more):
                steps = [0]

                def tick():
                    steps[0] += 1
                    return 1

                def feature_rows(t):
                    dve.wait_ge(ft_ps.sem, ft_ps.at(b, t + 1))
                    dve.tensor_tensor(feat[:, t, :, 0:U], bank[4 + t % 2][:].rearrange("p (h u) -> p h u", h=H),
                                      bias_bc[:].rearrange("p (h u) -> p h u", h=H), ALU.add).then_inc(ft_sb.sem, 1)

                x_low(b, 2)
                adj_rows(b, 2)
                feature_rows(0)
                x_low(b, 3)
                adj_rows(b, 3)
                feature_rows(1)
                adj_rows(b, 4)
                feature_rows(2)
                x_low(b, 4)
                x_low(b, 5)
                feature_rows(3)
                x_low(b, 6)
                x_low(b, 7)
                feature_rows(4)
                dve.wait_ge(sc_f32.sem, sc_f32.at(b, 2))
                dve.tensor_reduce(nmax16[:], sc_row[:], AX.X, ALU.max).then_inc(chain.sem, tick())
                dve.wait_ge(chain.sem, chain.at(b, steps[0]))
                dve.tensor_scalar(diag16[:], ident[0:SC, 0:SC], nmax16[:, 0:1], None,
                                  ALU.mult).then_inc(diag_ok.sem, 1)
                adj_rows(b, 5)
                dve.wait_ge(nat_ps.sem, nat_ps.at(b, 1))
                dve.tensor_copy(sc_nat[:], bank[7][:, 0:T * SC].rearrange("p (t s) -> p t s", t=T)).then_inc(
                    nat_sb.sem, 1)
                dve.wait_ge(nat_sb.sem, nat_sb.at(b, 1))
                dve.wait_ge(max_ps.sem, max_ps.at(b, 1))
                dve.tensor_copy(nmax[:], bank[6][:, 0:SC]).then_inc(chain.sem, tick())
                dve.wait_ge(chain.sem, chain.at(b, steps[0]))
                n_of = nmax[:, H:SC].unsqueeze(1).broadcast_to([P, T, H])
                dve.tensor_tensor(dn[:], sc_nat[:, :, H:SC], n_of, ALU.subtract).then_inc(weights_in.sem, 1)
                dve.tensor_tensor(ts[:], sc_nat[:, :, 0:H], n_of, ALU.add).then_inc(chain.sem, tick())
                dve.tensor_scalar(n_step[:], sc_nat[:, :, H:SC], STEP, None, ALU.mult).then_inc(weights_in.sem, 1)
                dve.wait_ge(chain.sem, chain.at(b, steps[0]))
                dve.tensor_scalar(ts_lo[:], ts[:], 0.0, None, ALU.min).then_inc(weights_in.sem, 1)
                dve.tensor_scalar(ts_hi[:], ts[:], 0.0, None, ALU.max).then_inc(weights_in.sem, 1)
                feature_rows(5)
                for s in range(2):
                    dve.wait_ge(y_stored[s], b * (16 * T // 2) + 16)
                dve.wait_ge(ft_sb.sem, ft_sb.at(b, HALF))
                dve.wait_ge(weights.sem, weights.at(b, 2))
                dve.wait_ge(ones_ok.sem, ones_ok.at(b, 1))
                value_f32_0(b)
                adj_rows(b, 6)
                adj_rows(b, 7)
                value_rest0(b, FIRST)
                dve.wait_ge(at_sb.sem, at_sb.at(b, T))

                def mask_upper(g):
                    h, jt = divmod(g, T)
                    dve.wait_ge(stepped.sem, stepped.at(b, g + 1))
                    if g >= MASK_SLOTS:
                        h0, j0 = divmod(g - MASK_SLOTS, T)
                        if j0 == T - 1:
                            dve.wait_ge(sums_ps.sem, sums_ps.at(b, (h0 + 1) * GROUPS))
                        else:
                            dve.wait_ge(mask_used.sem, mask_used.at(b, h0 * (T - 1) + j0 + 1))
                    dve.tensor_tensor(mask[:, 0, g % MASK_SLOTS], step[:, g % STEP_SLOTS], adj_t[:, jt, :],
                                      ALU.min).then_inc(mask1.sem, 1)

                def mask_lower(g):
                    h, jt = divmod(g, T)
                    if not lower_by[h, jt][0]:
                        dve.wait_ge(mask1.sem, mask1.at(b, g + 1))
                        dve.tensor_tensor(mask[:, 1, g % MASK_SLOTS], adj_t[:, jt, :], mask[:, 0, g % MASK_SLOTS],
                                          ALU.subtract).then_inc(mask2_dve.sem, 1)

                mask_upper(0)
                value_p2(b, 0, FIRST)
                feature_rows(6)
                mask_upper(1)
                mask_lower(1)
                feature_rows(7)
                mask_upper(2)
                mask_lower(2)
                mask_upper(3)
                value_rest0(b, SECOND)
                mask_lower(3)
                mask_upper(4)
                value_p2(b, 0, SECOND)
                mask_lower(4)
                mask_upper(5)
                mask_lower(5)

                def lower_at_once(g):
                    return g < T or g % T == T - 1

                for g in range(6, H * T):
                    h, jt = divmod(g, T)
                    mask_upper(g)
                    if not lower_at_once(g - 1):
                        mask_lower(g - 1)
                    if lower_at_once(g):
                        mask_lower(g)
                    if jt == 3 and h >= 1:
                        weigh_sums(b, h - 1)
                    if g == T - 1:
                        value_p2(b, 1)
                dve.wait_ge(head_ok.sem, head_ok.at(b, H - 1))
                dve.reciprocal(rden[:, :, 0:H - 1].unsqueeze(3), feat[:, :, 0:H - 1, U:U1]).then_inc(chain.sem, tick())

                def last_head_rows(i, tiles):
                    dve.wait_ge(weighted_ok.sem, weighted_ok.at(b, (H - 1) * GROUPS + (1 if i == 0 else GROUPS)))
                    dve.tensor_tensor(feat[:, tiles, H - 1, :], weighted[:, tiles, 0, :], weighted[:, tiles, 1, :],
                                      ALU.add).then_inc(last_head_ok.sem, 1)
                    dve.wait_ge(last_head_ok.sem, last_head_ok.at(b, i + 1))
                    dve.reciprocal(rden[:, tiles, H - 1:H].unsqueeze(3),
                                   feat[:, tiles, H - 1:H, U:U1]).then_inc(rden_ok.sem, 1)

                weigh_sums(b, H - 1, (0,))
                last_head_rows(0, slice(0, QPB))
                dve.wait_ge(chain.sem, chain.at(b, steps[0]))
                dve.wait_ge(rden_ok.sem, rden_ok.at(b, 1))
                dve.tensor_tensor(z[:, 0].rearrange("p (h u) -> p h u", h=H), feat[:, 0, :, 0:U],
                                  rden[:, 0, :].unsqueeze(2).broadcast_to([P, H, U]),
                                  ALU.mult).then_inc(ln0_norm.sem, 1)

                def ln0_residual(t):
                    dve.wait_ge(ln0_norm.sem, ln0_norm.at(b, t + 1))
                    dve.scalar_tensor_tensor(out=xs[:, t, :], in0=z[:, t % 2], scalar=0.0, in1=xs[:, t, :],
                                             op0=ALU.max, op1=ALU.add).then_inc(ln0_sum.sem, 1)

                def ln0_stats(t):
                    dve.wait_ge(ln0_sum.sem, ln0_sum.at(b, t + 1))
                    dve.bn_stats(stats[:, t % 2], xs[:, t, :]).then_inc(chain.sem, tick())
                    dve.wait_ge(chain.sem, chain.at(b, steps[0]))
                    stand(dve)
                    dve.bn_aggr(mv[:, t, :], stats[:, t % 2]).then_inc(ln0_mv.sem, 1)

                def ln0_factors(t):
                    dve.wait_ge(ln0_sd.sem, ln0_sd.at(b, t + 1))
                    dve.reciprocal(rs[:, t:t + 1], sd[:, t:t + 1]).then_inc(chain.sem, tick())
                    dve.wait_ge(chain.sem, chain.at(b, steps[0]))
                    dve.scalar_tensor_tensor(out=nb[:, t:t + 1], in0=mv[:, t, 0:1], scalar=-1.0, in1=rs[:, t:t + 1],
                                             op0=ALU.mult, op1=ALU.mult).then_inc(ln0_nb.sem, 1)

                def x1t_low(t):
                    dve.wait_ge(x1t_hi.sem, x1t_hi.at(b, t + 1))
                    dve.tensor_tensor(x1t_l[:], bank[5][:].rearrange("p (k n) -> p k n", k=KC),
                                      x1t_h[:].bitcast(F32), ALU.subtract).then_inc(x1t_lo.sem, 1)

                ln0_residual(0)
                for t in range(T):
                    ln0_stats(t)
                    if t + 1 < T:
                        ln0_residual(t + 1)
                    ln0_factors(t)
                    if t < 2:
                        weigh_sums(b, H - 1, (1 + t,))
                    if t == 0:
                        dve.wait_ge(deg_ps.sem, deg_ps.at(b, 1))
                        dve.tensor_scalar(degc[:], bank[7][:, 0:T], DEG_EPS, None, ALU.max).then_inc(deg_max.sem, 1)
                        dve.wait_ge(deg_max.sem, deg_max.at(b, 1))
                        dve.reciprocal(rdeg[:], degc[:]).then_inc(rdeg_ok.sem, 1)
                    if t == 1:
                        last_head_rows(1, slice(QPB, T))
                    if t == 4:
                        x1t_low(0)

                def ln1(t):
                    s = t % 2
                    if t >= 2:
                        dve.wait_ge(y_ok.sem, y_ok.at(b, t - 1))
                    if more and t == T - 1:
                        ones_column(b + 1)
                        adj_rows(b + 1, 0)
                    dve.wait_ge(o2_sb.sem, o2_sb.at(b, t + 1))
                    dve.tensor_tensor(z[:, s], bank[O1_BANKS[s]][:], o2s[:, s], ALU.add).then_inc(o_sum.sem, 1)
                    if more and t == T - 1:
                        x_low(b + 1, 0)
                    dve.wait_ge(o_sum.sem, o_sum.at(b, t + 1))
                    dve.scalar_tensor_tensor(out=z[:, s], in0=z[:, s], scalar=0.0, in1=xs[:, t, :],
                                             op0=ALU.max, op1=ALU.add).then_inc(res_ok.sem, 1)
                    dve.wait_ge(res_ok.sem, res_ok.at(b, t + 1))
                    dve.bn_stats(stats[:, s], z[:, s]).then_inc(chain.sem, tick())
                    dve.wait_ge(chain.sem, chain.at(b, steps[0]))
                    stand(dve)
                    dve.bn_aggr(mv1[:, s], stats[:, s]).then_inc(ln1_mv.sem, 1)

                def ln1_end(t):
                    s = t % 2
                    dve.wait_ge(ln1_sd.sem, ln1_sd.at(b, t + 1))
                    dve.reciprocal(rs1[:, s:s + 1], sd1[:, s:s + 1]).then_inc(chain.sem, tick())
                    dve.wait_ge(chain.sem, chain.at(b, steps[0]))
                    dve.wait_ge(y_stored[s], b * (16 * T // 2) + 16 * (t // 2) + 16)
                    dve.tensor_scalar(y_out[:, s], z[:, s], mv1[:, s, 0:1], rs1[:, s:s + 1],
                                      ALU.subtract, ALU.mult).then_inc(y_ok.sem, 1)

                def agg_low(half):
                    for f in range(KC):
                        dve.wait_ge(aggt_hi.sem, aggt_hi.at(b, half * KC + f + 1))
                        dve.tensor_tensor(trl[:, f, :], bank[AGG_BANKS[half][f]][:], trh[:, f, :].bitcast(F32),
                                          ALU.subtract).then_inc(aggt_lo.sem, 1)

                agg_low(0)
                x1t_low(1)
                for t in range(T):
                    if t == HALF - 1:
                        agg_low(1)
                        x1t_low(t + 2)
                    ln1(t)
                    if t + 2 < T and t != HALF - 1:
                        x1t_low(t + 2)
                    if t >= 1:
                        ln1_end(t - 1)
                if more:
                    adj_rows(b + 1, 1)
                    x_low(b + 1, 1)
                ln1_end(T - 1)
                assert steps[0] == chain.per_batch, steps

            dve.wait_ge(w_in[2], 16)
            ones_column(0)
            adj_rows(0, 0)
            x_low(0, 0)
            adj_rows(0, 1)
            x_low(0, 1)
            with dve.Fori(0, B - 1) as b:
                batch(b, True)
            batch(B - 1, False)

        @block.tensor
        def _(pe):
            def mm(o, l, r, start, stop):
                return pe.matmul(o, l, r, start=start, stop=stop, skip_group_check=True)

            pe.wait_ge(consts, 1)
            pe.wait_ge(w_in[3], 16)
            for f in range(2 * KC):
                if f >= 2:
                    pe.wait_ge(w1_lo, f - 1)
                for c in range(KC):
                    ins = pe.transpose(bank[f % 2][:, col(c)], sage_raw[:, c, f * P:(f + 1) * P], ident[:])
                ins.then_inc(w1_ps, 1)
            pe.wait_ge(w1_lo, 2 * KC)
            pe.wait_ge(w_ready, 4)
            pe.wait_ge(consts, N_CONST)

            def split_product(o, lh, ll, rh, rl, first=True, last=True):
                n = len(lh)
                for k in range(n):
                    for i, (a, c) in enumerate(((lh[k], rh[k]), (lh[k], rl[k]), (ll[k], rh[k]))):
                        ins = mm(o, a, c, first and k == 0 and i == 0, last and k == n - 1 and i == 2)
                return ins

            def turn_x(b, t):
                landed = x_in[t]
                pe.wait_ge(landed.sem, landed.at(b, 16))
                if t >= 2:
                    pe.wait_ge(xt_lo.sem, xt_lo.at(b, t - 1))
                for k in range(KC):
                    ins = pe.transpose(bank[t % 2][:, col(k)], xs[:, t, col(k)], ident[:])
                ins.then_inc(xt_ps.sem, 1)

            def turn_adj(b, t):
                pe.wait_ge(adj_cast.sem, adj_cast.at(b, t + 1))
                if t >= 2:
                    pe.wait_ge(at_sb.sem, at_sb.at(b, t - 1))
                for jt in range(T):
                    ins = pe.transpose(bank[ADJ_BANKS[t % 2]][:].bitcast(BF16)[:, col(jt)], adj_bf[:, t % 2, col(jt)],
                                       ident_bf[:])
                ins.then_inc(at_ps.sem, 1)

            def batch(b, more):
                def features(t):
                    pe.wait_ge(xt_lo.sem, xt_lo.at(b, t + 1))
                    if t >= 2:
                        pe.wait_ge(ft_sb.sem, ft_sb.at(b, t - 1))
                    c = t % HALF
                    split_product(bank[4 + t % 2][:], [trh[:, k, col(c)] for k in range(KC)],
                                  [trl[:, k, col(c)] for k in range(KC)], [w0h[:, k, :] for k in range(KC)],
                                  [w0l[:, k, :] for k in range(KC)]).then_inc(ft_ps.sem, 1)

                def scores(i):
                    pe.wait_ge(xt_lo.sem, xt_lo.at(b, (i + 1) * HALF))
                    if i == 1:
                        pe.wait_ge(sc_f32.sem, sc_f32.at(b, 1))
                    split_product(bank[6][:], [wah_wide[:, k * SC:k * SC + P] for k in range(KC)],
                                  [wal_wide[:, k * SC:k * SC + P] for k in range(KC)],
                                  [trh[:, k, :] for k in range(KC)],
                                  [trl[:, k, :] for k in range(KC)]).then_inc(sc_ps.sem, 1)

                turn_x(b, 2)
                turn_adj(b, 2)
                features(0)
                turn_x(b, 3)
                turn_adj(b, 3)
                features(1)
                turn_x(b, 4)
                turn_adj(b, 4)
                features(2)
                turn_x(b, 5)
                scores(0)
                features(3)
                turn_x(b, 6)
                turn_x(b, 7)
                features(4)
                scores(1)
                turn_adj(b, 5)
                pe.wait_ge(sc_f32.sem, sc_f32.at(b, 2))
                stand(pe)
                for t in range(T):
                    ins = pe.transpose(bank[7][:, t * SC:(t + 1) * SC], sc_row[:, col(t)], ident[0:SC, 0:SC])
                ins.then_inc(nat_ps.sem, 1)
                features(5)
                pe.wait_ge(diag_ok.sem, diag_ok.at(b, 1))
                mm(bank[6][:, 0:SC], ones16[:], diag16[:], True, True).then_inc(max_ps.sem, 1)
                turn_adj(b, 6)
                turn_adj(b, 7)

                def key_tile(h, jt, queries):
                    g = h * T + jt
                    by_pool, count = lower_by[h, jt]
                    lower_ok = mask2_pool if by_pool else mask2_dve
                    pe.wait_ge(lower_ok.sem, lower_ok.at(b, count))
                    pe.wait_ge(mask1.sem, mask1.at(b, g + 1))
                    for q in queries:
                        k, i = divmod(q, QPB)
                        for kind in range(2):
                            at = (2 * i + kind) * U1
                            for part in range(PARTS):
                                ins = mm(bank[3 * (h % 2) + k][:, at:at + U1],
                                         mask[:, kind, g % MASK_SLOTS, col(q)],
                                         val[:, h % 2, part, kind, jt, :],
                                         jt == 0 and i == 0 and kind == 0 and part == 0,
                                         jt == T - 1)
                        if jt == T - 1 and (i == QPB - 1 or q == T - 1):
                            ins.then_inc(sums_ps.sem, 1)
                    if jt < T - 1 and q == T - 1:
                        ins.then_inc(mask_used.sem, 1)

                features(6)
                features(7)
                for h in range(H):
                    if h < 2:
                        pe.wait_ge(val_p2.sem, val_p2.at(b, h + 2 if h else 1))
                    else:
                        pe.wait_ge(val_p2_pool.sem, val_p2_pool.at(b, h - 1))
                    if h >= 2:
                        pe.wait_ge(weighted_ok.sem, weighted_ok.at(b, (h - 1) * GROUPS))
                    for jt in range(T):
                        if h == 0 and jt == HALF:
                            pe.wait_ge(val_p2.sem, val_p2.at(b, 2))
                        if h < H - 1 or jt < T - EARLY:
                            key_tile(h, jt, range(T))
                        elif jt == T - 1:
                            for queries in (range(0, QPB), range(QPB, T)):
                                for late_jt in range(T - EARLY, T):
                                    key_tile(h, late_jt, queries)
                    if h == H - 1:
                        for q in range(T):
                            for jt in range(T):
                                ins = mm(bank[7][:, q:q + 1], adj_t[:, jt, col(q)], ones_bf[:], jt == 0, jt == T - 1)
                        ins.then_inc(deg_ps.sem, 1)

                def aggregate(half, f, jt, part):
                    r = (x1h, x1l)[part]
                    ins = mm(bank[AGG_BANKS[half][f]][:], r[:, jt, col(f)],
                             adj_t[:, jt, half * HALF * P:(half + 1) * HALF * P],
                             jt == 0 and part == 0, jt == T - 1 and part == 1)
                    if jt == T - 1 and part == 1:
                        ins.then_inc(agg_ps.sem, 1)

                def turn_x1(t):
                    if t >= 1:
                        pe.wait_ge(x1t_lo.sem, x1t_lo.at(b, t))
                    for k in range(KC):
                        ins = pe.transpose(bank[5][:, col(k)], xs[:, t, col(k)], ident[:])
                    ins.then_inc(x1t_ps.sem, 1)

                def own(t):
                    pe.wait_ge(x1t_lo.sem, x1t_lo.at(b, t + 1))
                    if t >= 2:
                        pe.wait_ge(o_sum.sem, o_sum.at(b, t - 1))
                    split_product(bank[O1_BANKS[t % 2]][:], [x1t_h[:, k, :] for k in range(KC)],
                                  [x1t_l[:, k, :] for k in range(KC)], [w1h[:, k, :] for k in range(KC)],
                                  [w1l[:, k, :] for k in range(KC)]).then_inc(o1_ps.sem, 1)

                def neighbours(t):
                    if t == 0:
                        pe.wait_ge(aggt_lo.sem, aggt_lo.at(b, KC))
                    else:
                        pe.wait_ge(o2_sb.sem, o2_sb.at(b, t))
                    at = col(t % HALF)
                    for k in range(KC):
                        if t == HALF:
                            pe.wait_ge(aggt_lo.sem, aggt_lo.at(b, KC + k + 1))
                        ins = split_product(bank[2][:], [trh[:, k, at]], [trl[:, k, at]], [w1h[:, KC + k, :]],
                                            [w1l[:, KC + k, :]], first=k == 0, last=k == KC - 1)
                    ins.then_inc(o2_ps.sem, 1)

                def aggregate_first(jt, part):
                    part_ok = (x1_hi, x1_lo)[part]
                    pe.wait_ge(part_ok.sem, part_ok.at(b, jt + 1))
                    for f in range(KC):
                        aggregate(0, f, jt, part)
                    if jt == 0 and part == 0:
                        pe.wait_ge(deg_max.sem, deg_max.at(b, 1))
                    for f in range(2):
                        aggregate(1, f, jt, part)

                for jt in range(T):
                    aggregate_first(jt, 0)
                    aggregate_first(jt, 1)
                    if jt == 1:
                        pe.wait_ge(weighted_ok.sem, weighted_ok.at(b, H * GROUPS))
                        turn_x1(0)
                    if jt == 4:
                        own(0)
                turn_x1(1)
                for t in range(T):
                    if t < 2:
                        pe.wait_ge(aggt_lo.sem, aggt_lo.at(b, t + 1))
                        for jt in range(T):
                            for part in range(2):
                                aggregate(1, 2 + t, jt, part)
                    neighbours(t)
                    if t + 1 < T:
                        own(t + 1)
                    if t + 2 < T:
                        turn_x1(t + 2)
                if more:
                    turn_adj(b + 1, 0)
                    turn_x(b + 1, 0)
                    turn_x(b + 1, 1)
                    pe.wait_ge(o2_sb.sem, o2_sb.at(b, T))
                    turn_adj(b + 1, 1)
                    pe.wait_ge(o_sum.sem, o_sum.at(b, T))

            turn_adj(0, 0)
            turn_x(0, 0)
            turn_x(0, 1)
            turn_adj(0, 1)
            with pe.Fori(0, B - 1) as b:
                batch(b, True)
            batch(B - 1, False)


_INS = ["x", "adj", "L0_gnn_W", "L0_gnn_b", "L0_gnn_a_self", "L0_gnn_a_neigh", "L1_gnn_W"]


def kernel(**inputs):
    import numpy as _np
    import concourse.bacc as _bacc
    from concourse import mybir as _mybir
    from concourse.bass_utils import run_bass_kernel_spmd as _run

    nc = _bacc.Bacc("TRN2", target_bir_lowering=False, num_devices=1)
    arrays, args = {}, []
    for name in _INS:
        a = _np.ascontiguousarray(inputs[name])
        arrays[f"in_{name}_dram"] = a
        args.append(nc.dram_tensor(f"in_{name}_dram", a.shape, _mybir.dt.from_np(a.dtype), kind="ExternalInput").ap())
    out = nc.dram_tensor("out_0_dram", inputs["x"].shape, _mybir.dt.float32, kind="ExternalOutput").ap()
    gat_sage_kernel(nc, *args, out)
    r = _run(nc, [arrays], core_ids=[0])
    return r.results[0]["out_0_dram"]
```
